# Optimizing a Trainium2 kernel written in Bass

```python
import numpy as np
import jax
import jax.numpy as jnp

def _softmax(x, axis=-1):
    return jax.nn.softmax(x, axis=axis)

def _gelu(x):
    return jax.nn.gelu(x, approximate=True)

def _silu(x):
    return jax.nn.silu(x)

def _sigmoid(x):
    return jax.nn.sigmoid(x)

def _layernorm(x, axis=-1, eps=1e-05):
    m = jnp.mean(x, axis=axis, keepdims=True)
    v = jnp.var(x, axis=axis, keepdims=True)
    return (x - m) / jnp.sqrt(v + eps)

def _scatter_add(tgt, idx, src, axis=0):
    return tgt.at[idx].add(src)

def _segment_sum(src, seg, n):
    return jax.ops.segment_sum(src, seg, n)
kernel_name = 'mk_xattn_seq_d4_seqx_r8_f48f55'

def setup_inputs(seed: int=0):
    np.random.seed(seed)
    _w = jnp.asarray

    def _rec_inputs():
        import jax
        import jax.numpy as jnp
        _rk = jax.random.key(seed)
        x = -0.0002928 + 1 * jax.random.normal(jax.random.fold_in(_rk, 1), (16, 128, 128), jnp.float32)
        _lenS = 128 - jax.random.randint(jax.random.fold_in(_rk, 7), (16,), 0, max(1, 128 // 4) + 1, jnp.int32)
        _lenS2 = 128 - jax.random.randint(jax.random.fold_in(_rk, 8), (16,), 0, max(1, 128 // 4) + 1, jnp.int32)
        _ctx_1024P = jax.random.normal(jax.random.fold_in(_rk, 11), (16, 16, 128), jnp.float32)
        _ctx_1024c = jax.random.dirichlet(jax.random.fold_in(_rk, 511), 0.3 * jnp.ones((16,), jnp.float32), (16, 128))
        _ctx_1024t = jnp.einsum('bsk,bkd->bsd', _ctx_1024c, _ctx_1024P)
        _ctx_1024t = _ctx_1024t * jax.lax.rsqrt(jnp.mean(jnp.square(_ctx_1024t)) + 1e-12) * 0.953939
        ctx_1024 = -1.52775e-05 + 0.999936 * (_ctx_1024t + 0.3 * jax.random.normal(jax.random.fold_in(_rk, 611), (16, 128, 128), jnp.float32))
        _validS = jnp.arange(128)[None, :] < _lenS[:, None]
        _validS2 = jnp.arange(128)[None, :] < _lenS2[:, None]
        _causal = jnp.tril(jnp.ones((128, 128), dtype=bool))
        mask_BxS2_bk1 = jnp.broadcast_to(_validS2[:, :], (16, 128))
        mask_1xS2_if1 = jnp.where(jnp.ones((1, 128), dtype=bool), 1, 0).astype(jnp.int32)
        return (x, ctx_1024, mask_BxS2_bk1, mask_1xS2_if1)
    x, ctx_1024, mask_BxS2_bk1, mask_1xS2_if1 = _rec_inputs()

    def _L0_xattn_setup():
        import jax, jax.numpy as jnp
        import numpy as np
        NUM_HEADS = 8
        QK_CH = 128
        V_CH = 128
        Q_DIM = 128
        KV_DIM = 128
        EPS = 1e-05

        def layernorm(x, w, b):
            mu = jnp.mean(x, axis=-1, keepdims=True)
            var = jnp.mean(jnp.square(x - mu), axis=-1, keepdims=True)
            return (x - mu) * jax.lax.rsqrt(var + EPS) * w + b
        key = jax.random.key(seed)
        ks = jax.random.split(key, 8)
        B, Q, K = (8, 64, 512)
        s = 0.02
        return {'hidden_states': jax.random.normal(ks[0], (B, Q, Q_DIM), jnp.float32), 'inputs': jax.random.normal(ks[1], (B, K, KV_DIM), jnp.float32), 'ln1_w': jnp.ones((Q_DIM,), jnp.float32), 'ln1_b': jnp.zeros((Q_DIM,), jnp.float32), 'ln2_w': jnp.ones((KV_DIM,), jnp.float32), 'ln2_b': jnp.zeros((KV_DIM,), jnp.float32), 'Wq': jax.random.normal(ks[2], (QK_CH, Q_DIM), jnp.float32) * s, 'bq': jnp.zeros((QK_CH,), jnp.float32), 'Wk': jax.random.normal(ks[3], (QK_CH, KV_DIM), jnp.float32) * s, 'bk': jnp.zeros((QK_CH,), jnp.float32), 'Wv': jax.random.normal(ks[4], (V_CH, KV_DIM), jnp.float32) * s, 'bv': jnp.zeros((V_CH,), jnp.float32)}
    _L0_xattn_all = _L0_xattn_setup()
    _L0_xattn_in = {k: v for k, v in _L0_xattn_all.items() if k in ('ln1_w', 'ln1_b', 'ln2_w', 'ln2_b', 'Wq', 'bq', 'Wk', 'bk', 'Wv', 'bv')}
    del _L0_xattn_all

    def _L1_xattn_setup():
        import jax, jax.numpy as jnp
        import numpy as np
        B, S, D, H = (2, 256, 128, 16)
        HD = D // H

        def _proj_split(x, W, b, n_heads):
            bsz, sq, dm = x.shape
            hd = dm // n_heads
            y = x @ W.T + b
            return y.reshape(bsz, sq, n_heads, hd).transpose(0, 2, 1, 3)
        key = jax.random.key(seed)
        ks = jax.random.split(key, 12)
        xav = (2.0 / (D + D)) ** 0.5
        q = jax.random.normal(ks[0], (B, S, D), jnp.float32)
        k = jax.random.normal(ks[1], (B, S, D), jnp.float32)
        v = jax.random.normal(ks[2], (B, S, D), jnp.float32)
        Wq = jax.random.normal(ks[3], (D, D), jnp.float32) * xav
        Wk = jax.random.normal(ks[4], (D, D), jnp.float32) * xav
        Wv = jax.random.normal(ks[5], (D, D), jnp.float32) * xav
        bq = jnp.zeros((D,), jnp.float32)
        bk = jnp.zeros((D,), jnp.float32)
        bv = jnp.zeros((D,), jnp.float32)
        klen = jax.random.randint(ks[6], (B,), S // 2, S + 1)
        qlen = jax.random.randint(ks[7], (B,), S // 2, S + 1)
        pos = jnp.arange(S)
        key_padding_mask = pos[None, :] < klen[:, None]
        query_padding_mask = pos[None, :] < qlen[:, None]
        return {'q': q, 'k': k, 'v': v, 'Wq': Wq, 'bq': bq, 'Wk': Wk, 'bk': bk, 'Wv': Wv, 'bv': bv, 'key_padding_mask': key_padding_mask, 'query_padding_mask': query_padding_mask}
    _L1_xattn_all = _L1_xattn_setup()
    _L1_xattn_in = {k: v for k, v in _L1_xattn_all.items() if k in ('Wq', 'bq', 'Wk', 'bk', 'Wv', 'bv')}
    del _L1_xattn_all

    def _L2_xattn_setup():
        import jax, jax.numpy as jnp
        import numpy as np
        DIM = 128
        NUM_HEADS = 16
        HEAD_DIM = DIM // NUM_HEADS
        FF = 4 * DIM
        B, T, S = (8, 64, 512)

        def _perceiver_layer(x, inp, Wq, bq, Wk, bk, Wv, bv, Wo, bo, W1, b1, W2, b2):
            b, t, _ = x.shape
            s = inp.shape[1]
            q = (x @ Wq + bq).reshape(b, t, NUM_HEADS, HEAD_DIM)
            k = (inp @ Wk + bk).reshape(b, s, NUM_HEADS, HEAD_DIM)
            v = (inp @ Wv + bv).reshape(b, s, NUM_HEADS, HEAD_DIM)
            attn = jnp.einsum('bthd,bshd->bhts', q, k)
            attn = jax.nn.softmax(attn / jnp.sqrt(jnp.float32(HEAD_DIM)), axis=-1)
            out = jnp.einsum('bhts,bshd->bthd', attn, v).reshape(b, t, DIM)
            attn_out = out @ Wo + bo
            x = x + attn_out
            h = jax.nn.gelu(x @ W1 + b1, approximate=True)
            x = x + (h @ W2 + b2)
            return x
        key = jax.random.key(seed)
        ks = jax.random.split(key, 14)
        sc = 1.0 / np.sqrt(DIM)
        inp = {'x': jax.random.normal(ks[0], (B, T, DIM), jnp.float32), 'inp': jax.random.normal(ks[1], (B, S, DIM), jnp.float32), 'Wq': jax.random.normal(ks[2], (DIM, DIM), jnp.float32) * sc, 'bq': jnp.zeros((DIM,), jnp.float32), 'Wk': jax.random.normal(ks[3], (DIM, DIM), jnp.float32) * sc, 'bk': jnp.zeros((DIM,), jnp.float32), 'Wv': jax.random.normal(ks[4], (DIM, DIM), jnp.float32) * sc, 'bv': jnp.zeros((DIM,), jnp.float32), 'Wo': jax.random.normal(ks[5], (DIM, DIM), jnp.float32) * sc, 'bo': jnp.zeros((DIM,), jnp.float32), 'W1': jax.random.normal(ks[6], (DIM, FF), jnp.float32) * sc, 'b1': jnp.zeros((FF,), jnp.float32), 'W2': jax.random.normal(ks[7], (FF, DIM), jnp.float32) * (1.0 / np.sqrt(FF)), 'b2': jnp.zeros((DIM,), jnp.float32)}
        return inp
    _L2_xattn_all = _L2_xattn_setup()
    _L2_xattn_in = {k: v for k, v in _L2_xattn_all.items() if k in ('Wq', 'bq', 'Wk', 'bk', 'Wv', 'bv', 'Wo', 'bo', 'W1', 'b1', 'W2', 'b2')}
    del _L2_xattn_all

    def _L3_xattn_setup():
        import jax, jax.numpy as jnp
        import numpy as np
        NEG = 10000000000.0

        def layer_norm(x, g, b, eps):
            m = jnp.mean(x, axis=-1, keepdims=True)
            v = jnp.mean(jnp.square(x - m), axis=-1, keepdims=True)
            return (x - m) * jax.lax.rsqrt(v + eps) * g + b

        def mha(q, k, v, mask, num_heads):
            B, T, E = q.shape
            S = k.shape[1]
            D = E // num_heads
            qh = q.reshape(B, T, num_heads, D).transpose(0, 2, 1, 3)
            kh = k.reshape(B, S, num_heads, D).transpose(0, 2, 1, 3)
            vh = v.reshape(B, S, num_heads, D).transpose(0, 2, 1, 3)
            scores = jnp.einsum('bhqd,bhkd->bhqk', qh, kh) * (1.0 / np.sqrt(D))
            scores = scores * mask - (1.0 - mask) * NEG
            attn = jax.nn.softmax(scores, axis=-1)
            out = jnp.einsum('bhqk,bhkd->bhqd', attn, vh)
            return out.transpose(0, 2, 1, 3).reshape(B, T, E)
        NUM_HEADS = 16
        key = jax.random.key(seed)
        ks = jax.random.split(key, 16)
        B, T, S, E, F, H = (1, 256, 256, 128, 512, 16)
        std = 0.02
        inp = {'target': jax.random.normal(ks[0], (B, T, E), jnp.float32), 'context': jax.random.normal(ks[1], (B, S, E), jnp.float32), 'target_pad_mask': jnp.ones((B, T), jnp.int32), 'context_pad_mask': jnp.ones((B, S), jnp.int32), 'Wqkv': jax.random.normal(ks[2], (E, 3 * E), jnp.float32) * std, 'Wo1': jax.random.normal(ks[3], (E, E), jnp.float32) * (std / np.sqrt(24.0)), 'bo1': jnp.zeros((E,), jnp.float32), 'g1': jnp.ones((E,), jnp.float32), 'b1': jnp.zeros((E,), jnp.float32), 'Wq': jax.random.normal(ks[4], (E, E), jnp.float32) * std, 'Wk': jax.random.normal(ks[5], (E, E), jnp.float32) * std, 'Wv': jax.random.normal(ks[6], (E, E), jnp.float32) * std, 'Wo2': jax.random.normal(ks[7], (E, E), jnp.float32) * (std / np.sqrt(24.0)), 'bo2': jnp.zeros((E,), jnp.float32), 'g2': jnp.ones((E,), jnp.float32), 'b2': jnp.zeros((E,), jnp.float32), 'W1': jax.random.normal(ks[8], (E, F), jnp.float32) * std, 'bf1': jnp.zeros((F,), jnp.float32), 'W2': jax.random.normal(ks[9], (F, E), jnp.float32) * std, 'bf2': jnp.zeros((E,), jnp.float32), 'g3': jnp.ones((E,), jnp.float32), 'b3': jnp.zeros((E,), jnp.float32)}
        return inp
    _L3_xattn_all = _L3_xattn_setup()
    _L3_xattn_in = {k: v for k, v in _L3_xattn_all.items() if k in ('Wqkv', 'Wo1', 'bo1', 'g1', 'b1', 'Wq', 'Wk', 'Wv', 'Wo2', 'bo2', 'g2', 'b2', 'W1', 'bf1', 'W2', 'bf2', 'g3', 'b3')}
    del _L3_xattn_all
    return {'x': x, 'ctx_1024': ctx_1024, 'mask_BxS2_bk1': mask_BxS2_bk1, 'mask_1xS2_if1': mask_1xS2_if1, 'L0_xattn_ln1_w': _L0_xattn_in['ln1_w'], 'L0_xattn_ln1_b': _L0_xattn_in['ln1_b'], 'L0_xattn_ln2_w': _L0_xattn_in['ln2_w'], 'L0_xattn_ln2_b': _L0_xattn_in['ln2_b'], 'L0_xattn_Wq': _L0_xattn_in['Wq'], 'L0_xattn_bq': _L0_xattn_in['bq'], 'L0_xattn_Wk': _L0_xattn_in['Wk'], 'L0_xattn_bk': _L0_xattn_in['bk'], 'L0_xattn_Wv': _L0_xattn_in['Wv'], 'L0_xattn_bv': _L0_xattn_in['bv'], 'L1_xattn_Wq': _L1_xattn_in['Wq'], 'L1_xattn_bq': _L1_xattn_in['bq'], 'L1_xattn_Wk': _L1_xattn_in['Wk'], 'L1_xattn_bk': _L1_xattn_in['bk'], 'L1_xattn_Wv': _L1_xattn_in['Wv'], 'L1_xattn_bv': _L1_xattn_in['bv'], 'L2_xattn_Wq': _L2_xattn_in['Wq'], 'L2_xattn_bq': _L2_xattn_in['bq'], 'L2_xattn_Wk': _L2_xattn_in['Wk'], 'L2_xattn_bk': _L2_xattn_in['bk'], 'L2_xattn_Wv': _L2_xattn_in['Wv'], 'L2_xattn_bv': _L2_xattn_in['bv'], 'L2_xattn_Wo': _L2_xattn_in['Wo'], 'L2_xattn_bo': _L2_xattn_in['bo'], 'L2_xattn_W1': _L2_xattn_in['W1'], 'L2_xattn_b1': _L2_xattn_in['b1'], 'L2_xattn_W2': _L2_xattn_in['W2'], 'L2_xattn_b2': _L2_xattn_in['b2'], 'L3_xattn_Wqkv': _L3_xattn_in['Wqkv'], 'L3_xattn_Wo1': _L3_xattn_in['Wo1'], 'L3_xattn_bo1': _L3_xattn_in['bo1'], 'L3_xattn_g1': _L3_xattn_in['g1'], 'L3_xattn_b1': _L3_xattn_in['b1'], 'L3_xattn_Wq': _L3_xattn_in['Wq'], 'L3_xattn_Wk': _L3_xattn_in['Wk'], 'L3_xattn_Wv': _L3_xattn_in['Wv'], 'L3_xattn_Wo2': _L3_xattn_in['Wo2'], 'L3_xattn_bo2': _L3_xattn_in['bo2'], 'L3_xattn_g2': _L3_xattn_in['g2'], 'L3_xattn_b2': _L3_xattn_in['b2'], 'L3_xattn_W1': _L3_xattn_in['W1'], 'L3_xattn_bf1': _L3_xattn_in['bf1'], 'L3_xattn_W2': _L3_xattn_in['W2'], 'L3_xattn_bf2': _L3_xattn_in['bf2'], 'L3_xattn_g3': _L3_xattn_in['g3'], 'L3_xattn_b3': _L3_xattn_in['b3']}

def reference(x, ctx_1024, mask_BxS2_bk1, mask_1xS2_if1, L0_xattn_ln1_w, L0_xattn_ln1_b, L0_xattn_ln2_w, L0_xattn_ln2_b, L0_xattn_Wq, L0_xattn_bq, L0_xattn_Wk, L0_xattn_bk, L0_xattn_Wv, L0_xattn_bv, L1_xattn_Wq, L1_xattn_bq, L1_xattn_Wk, L1_xattn_bk, L1_xattn_Wv, L1_xattn_bv, L2_xattn_Wq, L2_xattn_bq, L2_xattn_Wk, L2_xattn_bk, L2_xattn_Wv, L2_xattn_bv, L2_xattn_Wo, L2_xattn_bo, L2_xattn_W1, L2_xattn_b1, L2_xattn_W2, L2_xattn_b2, L3_xattn_Wqkv, L3_xattn_Wo1, L3_xattn_bo1, L3_xattn_g1, L3_xattn_b1, L3_xattn_Wq, L3_xattn_Wk, L3_xattn_Wv, L3_xattn_Wo2, L3_xattn_bo2, L3_xattn_g2, L3_xattn_b2, L3_xattn_W1, L3_xattn_bf1, L3_xattn_W2, L3_xattn_bf2, L3_xattn_g3, L3_xattn_b3):
    import jax
    import jax.numpy as jnp

    def _L0_xattn_ref(hidden_states, inputs, ln1_w, ln1_b, ln2_w, ln2_b, Wq, bq, Wk, bk, Wv, bv):
        import jax, jax.numpy as jnp
        import numpy as np
        NUM_HEADS = 8
        QK_CH = 128
        V_CH = 128
        Q_DIM = 128
        KV_DIM = 128
        EPS = 1e-05

        def layernorm(x, w, b):
            mu = jnp.mean(x, axis=-1, keepdims=True)
            var = jnp.mean(jnp.square(x - mu), axis=-1, keepdims=True)
            return (x - mu) * jax.lax.rsqrt(var + EPS) * w + b
        B, Qlen, _ = hidden_states.shape
        Klen = inputs.shape[1]
        H = NUM_HEADS
        dqk = QK_CH // H
        dv = V_CH // H
        h = layernorm(hidden_states, ln1_w, ln1_b)
        x = layernorm(inputs, ln2_w, ln2_b)
        q = (h @ Wq.T + bq).reshape(B, Qlen, H, dqk).transpose(0, 2, 1, 3)
        k = (x @ Wk.T + bk).reshape(B, Klen, H, dqk).transpose(0, 2, 1, 3)
        v = (x @ Wv.T + bv).reshape(B, Klen, H, dv).transpose(0, 2, 1, 3)
        scores = jnp.einsum('bhqd,bhkd->bhqk', q, k) / jnp.sqrt(jnp.float32(dqk))
        probs = jax.nn.softmax(scores, axis=-1)
        ctx = jnp.einsum('bhqk,bhkd->bhqd', probs, v)
        ctx = ctx.transpose(0, 2, 1, 3).reshape(B, Qlen, H * dv)
        return hidden_states + ctx

    def _L1_xattn_ref(q, k, v, Wq, bq, Wk, bk, Wv, bv, key_padding_mask, query_padding_mask):
        import jax, jax.numpy as jnp
        import numpy as np
        B, S, D, H = (2, 256, 128, 16)
        HD = D // H

        def _proj_split(x, W, b, n_heads):
            bsz, sq, dm = x.shape
            hd = dm // n_heads
            y = x @ W.T + b
            return y.reshape(bsz, sq, n_heads, hd).transpose(0, 2, 1, 3)
        bsz, sq, dm = q.shape
        sk = k.shape[1]
        Q = _proj_split(q, Wq, bq, H)
        K = _proj_split(k, Wk, bk, H)
        V = _proj_split(v, Wv, bv, H)
        scale = 1.0 / jnp.sqrt(jnp.asarray(Q.shape[-1], Q.dtype))
        scores = jnp.einsum('bhqd,bhkd->bhqk', Q, K) * scale
        scores = jnp.where(key_padding_mask[:, None, None, :], scores, -jnp.inf)
        causal_ok = jnp.tril(jnp.ones((sq, sk), bool))
        scores = jnp.where(causal_ok[None, None, :, :], scores, -jnp.inf)
        attn = jax.nn.softmax(scores, axis=-1)
        attn = jnp.where(query_padding_mask[:, None, :, None], attn, 0.0)
        out = jnp.einsum('bhqk,bhkd->bhqd', attn, V)
        out = out.transpose(0, 2, 1, 3).reshape(bsz, sq, dm)
        return out + q

    def _L2_xattn_ref(x, inp, Wq, bq, Wk, bk, Wv, bv, Wo, bo, W1, b1, W2, b2):
        import jax, jax.numpy as jnp
        import numpy as np
        DIM = 128
        NUM_HEADS = 16
        HEAD_DIM = DIM // NUM_HEADS
        FF = 4 * DIM
        B, T, S = (8, 64, 512)

        def _perceiver_layer(x, inp, Wq, bq, Wk, bk, Wv, bv, Wo, bo, W1, b1, W2, b2):
            b, t, _ = x.shape
            s = inp.shape[1]
            q = (x @ Wq + bq).reshape(b, t, NUM_HEADS, HEAD_DIM)
            k = (inp @ Wk + bk).reshape(b, s, NUM_HEADS, HEAD_DIM)
            v = (inp @ Wv + bv).reshape(b, s, NUM_HEADS, HEAD_DIM)
            attn = jnp.einsum('bthd,bshd->bhts', q, k)
            attn = jax.nn.softmax(attn / jnp.sqrt(jnp.float32(HEAD_DIM)), axis=-1)
            out = jnp.einsum('bhts,bshd->bthd', attn, v).reshape(b, t, DIM)
            attn_out = out @ Wo + bo
            x = x + attn_out
            h = jax.nn.gelu(x @ W1 + b1, approximate=True)
            x = x + (h @ W2 + b2)
            return x
        return _perceiver_layer(x, inp, Wq, bq, Wk, bk, Wv, bv, Wo, bo, W1, b1, W2, b2)

    def _L3_xattn_ref(target, context, target_pad_mask, context_pad_mask, Wqkv, Wo1, bo1, g1, b1, Wq, Wk, Wv, Wo2, bo2, g2, b2, W1, bf1, W2, bf2, g3, b3):
        import jax, jax.numpy as jnp
        import numpy as np
        NEG = 10000000000.0

        def layer_norm(x, g, b, eps):
            m = jnp.mean(x, axis=-1, keepdims=True)
            v = jnp.mean(jnp.square(x - m), axis=-1, keepdims=True)
            return (x - m) * jax.lax.rsqrt(v + eps) * g + b

        def mha(q, k, v, mask, num_heads):
            B, T, E = q.shape
            S = k.shape[1]
            D = E // num_heads
            qh = q.reshape(B, T, num_heads, D).transpose(0, 2, 1, 3)
            kh = k.reshape(B, S, num_heads, D).transpose(0, 2, 1, 3)
            vh = v.reshape(B, S, num_heads, D).transpose(0, 2, 1, 3)
            scores = jnp.einsum('bhqd,bhkd->bhqk', qh, kh) * (1.0 / np.sqrt(D))
            scores = scores * mask - (1.0 - mask) * NEG
            attn = jax.nn.softmax(scores, axis=-1)
            out = jnp.einsum('bhqk,bhkd->bhqd', attn, vh)
            return out.transpose(0, 2, 1, 3).reshape(B, T, E)
        NUM_HEADS = 16
        B, T, E = target.shape
        S = context.shape[1]
        tpad = target_pad_mask.astype(target.dtype)
        cpad = context_pad_mask.astype(target.dtype)
        causal = (jnp.arange(T)[:, None] >= jnp.arange(T)[None, :]).astype(target.dtype)
        self_mask = causal[None, None, :, :] * tpad[:, None, None, :]
        q, k, v = jnp.split(target @ Wqkv, 3, axis=-1)
        x = mha(q, k, v, self_mask, NUM_HEADS) @ Wo1 + bo1
        target = layer_norm(x + target, g1, b1, 1e-05)
        cross_mask = jnp.broadcast_to(cpad[:, None, None, :], (B, 1, 1, S))
        x = mha(target @ Wq, context @ Wk, context @ Wv, cross_mask, NUM_HEADS) @ Wo2 + bo2
        target = layer_norm(x + target, g2, b2, 1e-05)
        h = jax.nn.gelu(target @ W1 + bf1, approximate=False)
        x = h @ W2 + bf2
        return layer_norm(x + target, g3, b3, 1e-06)
    x = _L0_xattn_ref(x, ctx_1024, L0_xattn_ln1_w, L0_xattn_ln1_b, L0_xattn_ln2_w, L0_xattn_ln2_b, L0_xattn_Wq, L0_xattn_bq, L0_xattn_Wk, L0_xattn_bk, L0_xattn_Wv, L0_xattn_bv)
    x = _L1_xattn_ref(x, ctx_1024, ctx_1024, L1_xattn_Wq, L1_xattn_bq, L1_xattn_Wk, L1_xattn_bk, L1_xattn_Wv, L1_xattn_bv, mask_BxS2_bk1, mask_BxS2_bk1)
    x = _L2_xattn_ref(x, ctx_1024, L2_xattn_Wq, L2_xattn_bq, L2_xattn_Wk, L2_xattn_bk, L2_xattn_Wv, L2_xattn_bv, L2_xattn_Wo, L2_xattn_bo, L2_xattn_W1, L2_xattn_b1, L2_xattn_W2, L2_xattn_b2)
    x = _L3_xattn_ref(x, ctx_1024, mask_1xS2_if1, mask_1xS2_if1, L3_xattn_Wqkv, L3_xattn_Wo1, L3_xattn_bo1, L3_xattn_g1, L3_xattn_b1, L3_xattn_Wq, L3_xattn_Wk, L3_xattn_Wv, L3_xattn_Wo2, L3_xattn_bo2, L3_xattn_g2, L3_xattn_b2, L3_xattn_W1, L3_xattn_bf1, L3_xattn_W2, L3_xattn_bf2, L3_xattn_g3, L3_xattn_b3)
    return x

_drawn_inputs = setup_inputs


def setup_inputs(seed=0):
    import zlib

    import numpy as np

    out = dict(_drawn_inputs(seed))
    spreads = {'L0_xattn_ln1_w': (1.0, 0.6),
     'L0_xattn_ln1_b': (0.0, 0.8),
     'L0_xattn_ln2_w': (1.0, 0.6),
     'L0_xattn_ln2_b': (0.0, 0.4),
     'L0_xattn_bq': (0.0, 0.8),
     'L0_xattn_bk': (0.0, 0.8),
     'L0_xattn_bv': (0.0, 0.1),
     'L1_xattn_bq': (0.0, 0.441),
     'L1_xattn_bk': (0.0, 0.8),
     'L1_xattn_bv': (0.0, 0.1),
     'L2_xattn_bq': (0.0, 0.463),
     'L2_xattn_bk': (0.0, 0.8),
     'L2_xattn_bv': (0.0, 0.1),
     'L2_xattn_bo': (0.0, 0.1),
     'L2_xattn_b1': (0.0, 0.1),
     'L2_xattn_b2': (0.0, 0.1),
     'L3_xattn_bo1': (0.0, 0.1),
     'L3_xattn_g1': (1.0, 0.2),
     'L3_xattn_b1': (0.0, 0.1),
     'L3_xattn_bo2': (0.0, 0.1),
     'L3_xattn_g2': (1.0, 0.2),
     'L3_xattn_b2': (0.0, 0.1),
     'L3_xattn_bf1': (0.0, 0.395),
     'L3_xattn_bf2': (0.0, 0.1),
     'L3_xattn_g3': (1.0, 0.2),
     'L3_xattn_b3': (0.0, 0.1)}
    factors = {'L0_xattn_Wq': 8.0,
     'L0_xattn_Wk': 8.0,
     'L3_xattn_Wqkv': 8.0,
     'L3_xattn_Wo1': 8.0,
     'L3_xattn_Wq': 8.0,
     'L3_xattn_Wk': 8.0,
     'L3_xattn_Wv': 8.0,
     'L3_xattn_Wo2': 8.0}
    for name, (base, spread) in spreads.items():
        noise = np.random.default_rng([zlib.crc32(name.encode()), seed]).standard_normal(out[name].shape)
        drawn = base * np.exp(spread * noise) if base else spread * noise
        out[name] = jnp.asarray(drawn.astype(out[name].dtype))
    for name, factor in factors.items():
        out[name] = (out[name] * factor).astype(out[name].dtype)
    return out
```

```python
from collections import namedtuple
from contextlib import ExitStack

import concourse.bass as bass
from concourse import mybir

F32 = mybir.dt.float32
BF16 = mybir.dt.bfloat16
U32 = mybir.dt.uint32
I32 = mybir.dt.int32
U8 = mybir.dt.uint8
ALU = mybir.AluOpType
ACT = mybir.ActivationFunctionType
AX_X = mybir.AxisListType.X

P = 128
BATCHES, S, D, FF = 16, 128, 128, 512
PAIR = 2
SETS = 4
GROUP = PAIR * SETS
ITERS = BATCHES // GROUP
TOK = PAIR * S
PARTS = 5
L0, L1, L2, L3S, L3C = range(PARTS)
HEADS = (8, 16, 16, 16, 16)
UNITS = PARTS * SETS
STACK = 96
TERMS = 3
ROWS = STACK + TERMS
PRODUCTS = ((0, 0), (0, 1), (1, 0), (0, 2), (2, 0), (1, 1))
BIG = float(2 ** 100)
RING = 3
SLOT = 8
EPS_LN, EPS_LAST = 1e-5, 1e-6

W_NAMES = ([f"{m}{p}" for p in range(PARTS) for m in "qkv"] + ["o2", "o3", "o4"]
           + [f"w1_{l}_{c}" for l in (2, 4) for c in range(4)] + [f"w2_{l}_{c}" for l in (2, 4) for c in range(4)])
W_AT = {n: i for i, n in enumerate(W_NAMES)}
W_FIRST = 3
C_NAMES = ["ln1_w", "ln1_b", "ln2_w", "ln2_b", "bq0", "bk0", "bq1", "bk1", "bq2", "bk2", "bo2", "bo3", "bo4",
           "m2_2", "m2_4", "g3", "b3", "g4", "b4"] + [f"m1_{l}_{c}" for l in (2, 4) for c in range(4)]
C_AT = {n: i for i, n in enumerate(C_NAMES)}
R_NAMES = ["bv0", "bv1", "bv2", "g5", "b5"]
R_AT = {n: i for i, n in enumerate(R_NAMES)}

QK_AT = {L0: -3, L1: -4, L2: -4, L3S: 0, L3C: 0}

Step = namedtuple("Step", "kind u b g")
MISC = {"raw_tr": "act", "ln_tr": "act", "qk": "act", "v": "dve", "n_tr": "dve", "o_tr": "dve", "a_tr": "dve",
        "wo": "dve", "w1": "act", "w2": "dve", "x_tr": "dve", "x_back": "dve"}


def schedule():
    at = {}

    def put(slot, pos, rank, step):
        at.setdefault((slot * SLOT + pos, rank, len(at)), step)

    for u in range(UNITS):
        part = u // SETS
        banks = HEADS[part] // 4
        every = 4 // banks
        if part == L0:
            for pos, kind in ((-6, "ln_in"), (-6, "raw_tr"), (-4, "ln_tr"), (-3, "qk"), (-3, "split"), (1, "v")):
                put(u - 2, pos, 2, Step(kind, u, 0, 0))
        else:
            first = QK_AT[part]
            for pos, kind in ((first, "qk"), (first, "split"), (1, "v")):
                put(u - 2, pos, 2, Step(kind, u, 0, 0))
        first = QK_AT[part]
        for c in range(len(PRODUCTS)):
            put(u - 2, first + 4 + c // 2, 2, Step("stack", u, c, 0))
        for b in range(PAIR):
            for g in range(banks):
                pos = 4 * b + every * g
                put(u - 1, pos, 1, Step("score", u, b, g))
                put(u, pos, 0, Step("attn", u, b, g))
                put(u, pos + 1, 0.5, Step("pv", u, b, g))
            last = 4 * b + every * (banks - 1)
            put(u - 1, last, 1.1, Step("nmax", u, b, 0))
            put(u - 1, last + 2, 1.5, Step("n_tr", u, b, 0))
            put(u, last + 1, 0.6, Step("o_evac", u, b, 0))
            put(u, last + 2, 1.6, Step("o_tr", u, b, 0))
        chain = {L0: [(2, "a_tr")], L1: [(2, "a_tr")],
                 L2: [(2, "a_tr"), (3, "wo"), (4, "w1"), (4, "w1"), (6, "w2")],
                 L3S: [(2, "a_tr"), (3, "wo"), (4, "x_tr"), (6, "x_back")],
                 L3C: [(2, "a_tr"), (3, "wo"), (4, "x_tr"), (6, "x_back"), (8, "w1"), (8, "w1"), (10, "w2"),
                       (12, "x_tr"), (12, "out")]}[part]
        seen = {}
        for pos, kind in chain:
            seen[kind] = seen.get(kind, -1) + 1
            put(u + 1, pos, 3, Step(kind, u, seen[kind], 0))
    return [at[k] for k in sorted(at)]


STEPS = schedule()


def numbering():
    count, num, evac, before, last = {}, {}, {}, {}, {}
    steps = [s for s in STEPS if s.kind in MISC]
    for n, s in enumerate(steps):
        last[n % 2] = s
    wrapped = dict(last)
    last = {}
    for n, s in enumerate(steps):
        e = MISC[s.kind]
        evac[s] = count.get(e, 0)
        count[e] = evac[s] + 1
        bank = n % 2
        before[s] = (bank, last.get(bank, wrapped[bank]), bank in last, n)
        last[bank] = s
    for s in STEPS:
        num[s] = count.get(s.kind, 0)
        count[s.kind] = num[s] + 1
    return count, num, evac, before


COUNT, NUM, EVAC, BEFORE = numbering()
X_WRITES = [s for s in STEPS if s.kind in ("wo", "w2", "x_back") or (s.kind == "a_tr" and s.u // SETS <= L1)]
LN_STEPS = [s for s in STEPS if s.kind in ("ln_in", "x_tr")]
N_LN = len(LN_STEPS)


def x_written_before(step):
    found = None
    for s in STEPS[:STEPS.index(step)]:
        if s in X_WRITES and s.u % SETS == step.u % SETS:
            found = s
    return found


def build(nc, x, ctx_in, weights, cols, rows, valid, valid_t, pad, pad_t, out):
    with ExitStack() as stack:
        def sb(name, shape, dt=F32):
            return stack.enter_context(nc.sbuf_tensor(name, shape, dt))

        def sem(name):
            return stack.enter_context(nc.semaphore(name))

        w = sb("w", [P, len(W_NAMES), P])
        col = sb("col", [P, len(C_NAMES)])
        bq_scaled = sb("bq_scaled", [P, 3])
        row = sb("row", [P, len(R_NAMES), P])
        ident = sb("ident", [P, P])
        ident_bf = sb("ident_bf", [P, P], BF16)
        causal_t = sb("causal_t", [P, S], BF16)
        valid_raw = sb("valid_raw", [P, GROUP, S], U8)
        valid_neg = sb("valid_neg", [P, GROUP, S], BF16)
        mask_l1 = sb("mask_l1", [P, GROUP, S], BF16)
        validt_raw = sb("validt_raw", [P, BATCHES], U8)
        valid_col = sb("valid_col", [P, BATCHES])
        keep_l1 = sb("keep_l1", [P, GROUP])
        bias_l1 = sb("bias_l1", [P, GROUP])
        pad_raw = sb("pad_raw", [P, S], I32)
        padt_raw = sb("padt_raw", [P, 1], I32)
        pad_neg = sb("pad_neg", [P, S], BF16)
        pad_bias = sb("pad_bias", [P, 1])
        mask_l3 = sb("mask_l3", [P, S], BF16)
        mask_l3_t = sb("mask_l3_t", [P, S], BF16)
        one_rows = sb("one_rows", [P, TOK], BF16)
        zero_rows = sb("zero_rows", [STACK // 2, 2 * TOK], BF16)
        minus_half = sb("minus_half", [P, 4])

        x_tok = [sb(f"x_tok{s}", [P, PAIR, D]) for s in range(SETS)]
        c_tok = [sb(f"c_tok{s}", [P, PAIR, D]) for s in range(SETS)]
        xT = [sb(f"xT{s}", [P, TOK]) for s in range(SETS)]
        cT = [sb(f"cT{s}", [P, TOK]) for s in range(SETS)]
        y = [sb(f"y{s}", [P, PAIR, D]) for s in range(SETS)]
        hT = sb("hT", [P, TOK])
        cnT = sb("cnT", [P, TOK])
        stats = sb("stats", [P, 2 * PAIR, 6])
        mean_var = sb("mean_var", [P, 2 * PAIR, 2])
        var_eps = sb("var_eps", [P, 2 * PAIR])
        rstd = sb("rstd", [P, 2 * PAIR])
        normed_in = sb("normed_in", [P, 2 * PAIR, D])
        normed = sb("normed", [P, PAIR, D])
        qk_f32 = sb("qk_f32", [P, 2, TOK])
        rest = sb("rest", [P, 2, TOK])
        terms_ring = [sb(f"terms{r}", [P, 2, TERMS, TOK], BF16) for r in range(2)]
        pairs8 = [sb(f"pairs8_{r}", [P, 8, 2, TOK], BF16) for r in range(RING)]
        pairs16 = [sb(f"pairs16_{r}", [P, 16, 2, TOK], BF16) for r in range(RING)]
        v8 = [sb(f"v8_{r}", [P, PAIR * 8 * 17 + 16]) for r in range(RING)]
        v16 = [sb(f"v16_{r}", [P, PAIR * 16 * 9 + 24]) for r in range(RING)]
        negmax = [sb(f"negmax{r}", [P, 16]) for r in range(2)]
        negmax_rest = [sb(f"negmax_rest{r}", [P, 16]) for r in range(2)]
        max_terms = [sb(f"max_terms{r}", [P, P], BF16) for r in range(2)]
        max_rows = [sb(f"max_rows{r}", [TERMS * 16, S], BF16) for r in range(4)]
        probs = [sb(f"probs{r}", [P, 4, S]) for r in range(3)]
        o_sb = [sb(f"o_sb{r}", [P, 512]) for r in range(2)]
        recip = sb("recip", [P, 16])
        attn_tok = sb("attn_tok", [P, PAIR, D])
        attnT = sb("attnT", [P, TOK])
        hidden = sb("hidden", [P, 4, TOK])

        score_ps = [stack.enter_context(nc.psum_tensor(f"score_ps{r}", [P, 512], F32)) for r in range(2)]
        attn_ps = [stack.enter_context(nc.psum_tensor(f"attn_ps{r}", [P, 512], F32)) for r in range(2)]
        o_ps = [stack.enter_context(nc.psum_tensor(f"o_ps{r}", [P, 512], F32)) for r in range(2)]
        misc_ps = [stack.enter_context(nc.psum_tensor(f"misc_ps{r}", [P, 512], F32)) for r in range(2)]

        first_landed = sem("first_landed")
        weights_landed = sem("weights_landed")
        masks_landed = sem("masks_landed")
        tokens_landed = [sem(f"tokens_landed{s}") for s in range(SETS)]
        valid_landed = sem("valid_landed")
        stack_landed = [sem(f"stack_landed{r}") for r in range(RING)]
        max_landed = [sem(f"max_landed{r}") for r in range(2)]
        out_landed = sem("out_landed")
        pool_const = sem("pool_const")
        dve_const = sem("dve_const")
        masks_ready = sem("masks_ready")
        fill_landed = sem("fill_landed")
        pool_mask = sem("pool_mask")
        wait_passed = sem("wait_passed")
        misc_ready = sem("misc_ready")
        evac = {"act": sem("evac_act"), "dve": sem("evac_dve")}
        score_ready = sem("score_ready")
        score_reduced = sem("score_reduced")
        term1_done = sem("term1_done")
        maxrest_done = sem("maxrest_done")
        term2_done = sem("term2_done")
        maxterms_ready = sem("maxterms_ready")
        attn_ready = sem("attn_ready")
        exp_done = sem("exp_done")
        pv_done = sem("pv_done")
        o_saved = sem("o_saved")
        recip_done = sem("recip_done")
        stats_done = sem("stats_done")
        var_ready = sem("var_ready")
        eps_added = sem("eps_added")
        rstd_ready = sem("rstd_ready")
        input_normed = sem("input_normed")
        split1_done = sem("split1_done")
        split2_done = sem("split2_done")
        split_done = sem("split_done")
        scaled_g = sem("scaled_g")
        y_ready = sem("y_ready")

        def reached(i, per, n):
            return (i + 1) * per + n + 1

        def evacuated(eng, i, step, earlier=False):
            e = MISC[step.kind]
            eng.wait_ge(evac[e], reached(i, COUNT[e], EVAC[step] - (COUNT[e] if earlier else 0)))

        def alone(eng):
            eng.sem_inc(wait_passed, 1)

        N_MISC = sum(COUNT[k] for k in MISC)
        N_SCORE = COUNT["score"]
        N_UB = UNITS * PAIR

        def ub(s):
            return s.u * PAIR + s.b

        def stack_of(u):
            return (pairs8 if u // SETS == L0 else pairs16)[u % RING]

        def v_of(u):
            return (v8 if u // SETS == L0 else v16)[u % RING]

        def stacks_per_iteration(r):
            return len([u for u in range(UNITS) if u % RING == r])

        def stacked(eng, i, u):
            back = u < 0
            u %= UNITS
            per = stacks_per_iteration(u % RING)
            eng.wait_ge(stack_landed[u % RING], ((i + (0 if back else 1)) * per + u // RING + 1) * 16 * len(PRODUCTS))

        def the(kind, u, b=0, g=0):
            return Step(kind, u, b, g)

        block = stack.enter_context(nc.Block())

        @block.sync
        def _(sp):
            sp.dma_start(w[:, 0:W_FIRST, :], weights[:, 0:W_FIRST, :]).then_inc(first_landed, 16)
            sp.dma_start(col[:, :], cols).then_inc(first_landed, 16)
            sp.dma_start(row[:, :, :], rows.partition_broadcast(P)).then_inc(first_landed, 16)
            for r in range(2):
                sp.sem_inc(max_landed[r], 16 * N_UB // 2)
            for r in range(RING):
                sp.sem_inc(stack_landed[r], 16 * len(PRODUCTS) * stacks_per_iteration(r))
            with sp.Fori(0, ITERS) as i:
                for s in range(SETS):
                    evacuated(sp, i, the("ln_tr", s), earlier=True)
                    alone(sp)
                    first = i * GROUP + s * PAIR
                    sp.dma_start(x_tok[s][:, :, :], x[bass.ds(first, PAIR)].rearrange("b t d -> t b d"))\
                        .then_inc(tokens_landed[s], 16)
                    sp.dma_start(c_tok[s][:, :, :], ctx_in[bass.ds(first, PAIR)].rearrange("b t d -> t b d"))\
                        .then_inc(tokens_landed[s], 16)
                for step in STEPS:
                    u = step.u
                    heads = HEADS[u // SETS]
                    if step.kind == "stack":
                        c = step.b
                        if c == 0:
                            sp.wait_ge(split_done, reached(i, UNITS, u))
                            alone(sp)
                            sp.wait_ge(o_saved, reached(i, N_UB, (u - RING) * PAIR + PAIR - 1))
                        d = D // heads
                        tq, tk = PRODUCTS[c]
                        terms = terms_ring[u % 2]
                        gap = TERMS + tk - tq
                        sp.dma_start(stack_of(u)[c * d:(c + 1) * d, :, :, :],
                                     terms[:, :, :, :].rearrange("p a t n -> p (a t) n")[:, tq:tq + gap + 1:gap, :])\
                            .then_inc(stack_landed[u % RING], 16)
                    if step.kind == "n_tr":
                        evacuated(sp, i, step)
                        n = ub(step)
                        sp.dma_start(stack_of(u)[STACK:ROWS, :, 0, step.b * S:(step.b + 1) * S],
                                     max_rows[n % 4][0:TERMS * heads, :]).then_inc(max_landed[n % 2], 16)

        @block.gpsimd
        def _(pool):
            pool.dma_start(padt_raw[:, :], pad_t).then_inc(masks_landed, 16)
            pool.dma_start(pad_raw[:, :], pad.partition_broadcast(P)).then_inc(masks_landed, 16)
            pool.dma_start(validt_raw[:, :], valid_t).then_inc(masks_landed, 16)
            pool.dma_start(w[:, W_FIRST:, :], weights[:, W_FIRST:, :]).then_inc(weights_landed, 16)
            pool.memset(one_rows[:, :], 1.0).then_inc(pool_const, 1)
            pool.memset(zero_rows[:, :], 0.0).then_inc(pool_const, 1)
            pool.memset(ident[:, :], 0.0).then_inc(pool_const, 1)
            pool.memset(causal_t[:, :], 0.0).then_inc(pool_const, 1)
            pool.memset(minus_half[:, :], -0.5).then_inc(pool_const, 1)
            pool.wait_ge(pool_const, 5)
            pool.affine_select(out=ident[:, :], in_=ident[:, :], compare_op=ALU.not_equal, fill=1.0, base=0,
                               pattern=[[-1, P]], channel_multiplier=1).then_inc(pool_const, 1)
            pool.affine_select(out=causal_t[:, :], in_=causal_t[:, :], compare_op=ALU.is_ge, fill=-BIG, base=0,
                               pattern=[[1, S]], channel_multiplier=-1).then_inc(pool_const, 1)
            pool.wait_ge(pool_const, 7)
            pool.tensor_copy(ident_bf[:, :], ident[:, :]).then_inc(pool_const, 1)
            pool.wait_ge(masks_landed, 48)
            pool.tensor_scalar(pad_neg[:, :], pad_raw[:, :], 1.0, BIG, ALU.subtract, ALU.mult).then_inc(pool_mask, 1)
            pool.tensor_scalar(pad_bias[:, :], padt_raw[:, :], 1.0, BIG, ALU.subtract, ALU.mult)\
                .then_inc(pool_mask, 1)
            pool.tensor_copy(valid_col[:, :], validt_raw[:, :]).then_inc(pool_mask, 1)
            pool.wait_ge(pool_mask, 3)
            pool.affine_select(out=mask_l3[:, :], in_=pad_neg[:, :], compare_op=ALU.is_ge, fill=-BIG, base=0,
                               pattern=[[-1, S]], channel_multiplier=1).then_inc(pool_const, 1)
            pool.tensor_scalar(mask_l3_t[:, :], causal_t[:, :], pad_bias[:, 0:1], None, ALU.min)\
                .then_inc(pool_const, 1)
            for s_, per in ((eps_added, N_LN), (rstd_ready, N_LN), (split2_done, UNITS),
                            (split_done, UNITS), (scaled_g, SETS), (y_ready, SETS), (masks_ready, 3)):
                pool.sem_inc(s_, per)
            with pool.Fori(0, ITERS) as i:
                pool.dma_start(valid_raw[:, :, :], valid[bass.ds(i * GROUP, GROUP)].partition_broadcast(P))\
                    .then_inc(valid_landed, 16)
                pool.tensor_copy(keep_l1[:, :], valid_col[:, bass.ds(i * GROUP, GROUP)]).then_inc(masks_ready, 1)
                pool.wait_ge(masks_ready, reached(i, 3, 0))
                alone(pool)
                pool.tensor_scalar(bias_l1[:, :], keep_l1[:, :], 1.0, BIG, ALU.subtract, ALU.mult)\
                    .then_inc(masks_ready, 1)
                masked = False
                for step in STEPS:
                    u = step.u
                    if step.kind == "split" and u == 1:
                        masked = True
                        pool.wait_ge(valid_landed, 16 * (i + 1))
                        alone(pool)
                        pool.tensor_scalar(valid_neg[:, :, :], valid_raw[:, :, :], 1.0, BIG, ALU.subtract, ALU.mult)\
                            .then_inc(pool_mask, 1)
                        pool.wait_ge(pool_mask, i + 4)
                        alone(pool)
                        pool.affine_select(out=mask_l1[:, :, :], in_=valid_neg[:, :, :], compare_op=ALU.is_ge,
                                           fill=-BIG, base=0, pattern=[[0, GROUP], [-1, S]],
                                           channel_multiplier=1).then_inc(masks_ready, 1)
                    if step in LN_STEPS:
                        n = LN_STEPS.index(step)
                        k = 2 * PAIR if step.kind == "ln_in" else PAIR
                        eps = EPS_LAST if step.kind == "x_tr" and step.b == 1 else EPS_LN
                        pool.wait_ge(var_ready, reached(i, N_LN, n))
                        alone(pool)
                        pool.tensor_scalar(var_eps[:, 0:k], mean_var[:, 0:k, 1], eps, None, ALU.add)\
                            .then_inc(eps_added, 1)
                        pool.wait_ge(eps_added, reached(i, N_LN, n))
                        pool.tensor_tensor(rstd[:, 0:k], var_eps[:, 0:k], minus_half[:, 0:k], ALU.pow)\
                            .then_inc(rstd_ready, 1)
                    if step.kind == "split":
                        terms = terms_ring[u % 2]
                        pool.wait_ge(split1_done, reached(i, UNITS, u))
                        pool.tensor_tensor(rest[:, :, :], qk_f32[:, :, :], terms[:, :, 0, :], ALU.subtract)
                        pool.tensor_tensor(terms[:, :, 1, :], qk_f32[:, :, :], terms[:, :, 0, :], ALU.subtract)\
                            .then_inc(split2_done, 1)
                        pool.wait_ge(split2_done, reached(i, UNITS, u))
                        pool.tensor_tensor(terms[:, :, 2, :], rest[:, :, :], terms[:, :, 1, :], ALU.subtract)\
                            .then_inc(split_done, 1)
                    if step.kind == "out":
                        s = u % SETS
                        evacuated(pool, i, the("x_tr", u, 1))
                        pool.tensor_tensor(y[s][:, :, :], normed[:, :, :],
                                           row[:, R_AT["g5"], :].unsqueeze(1).to_broadcast([P, PAIR, D]),
                                           ALU.mult).then_inc(scaled_g, 1)
                        pool.wait_ge(scaled_g, reached(i, SETS, s))
                        pool.tensor_tensor(y[s][:, :, :], y[s][:, :, :],
                                           row[:, R_AT["b5"], :].unsqueeze(1).to_broadcast([P, PAIR, D]),
                                           ALU.add).then_inc(y_ready, 1)
                        pool.wait_ge(y_ready, reached(i, SETS, s))
                        alone(pool)
                        pool.dma_start(out[bass.ds(i * GROUP + s * PAIR, PAIR)].rearrange("b t d -> t b d"),
                                       y[s][:, :, :]).then_inc(out_landed, 16)
                pool.wait_ge(out_landed, 16 * SETS * (i + 1))
                alone(pool)

        @block.scalar
        def _(act):
            act.sem_inc(evac["act"], COUNT["act"])
            act.sem_inc(exp_done, N_SCORE)
            act.sem_inc(o_saved, N_UB)
            act.wait_ge(pool_const, 2)
            for r in range(RING):
                for pairs, heads in ((pairs8[r], 8), (pairs16[r], 16)):
                    act.dma_start(pairs[STACK:ROWS, :, 1, :],
                                  one_rows[0:TERMS, :].unsqueeze(1).to_broadcast([TERMS, heads, TOK]))\
                        .then_inc(fill_landed, 16)
                act.dma_start(pairs16[r][STACK // 2:STACK, :, :, :].rearrange("p h a n -> p h (a n)"),
                              zero_rows[:, :].unsqueeze(1).to_broadcast([STACK // 2, 16, 2 * TOK]))\
                    .then_inc(fill_landed, 16)
            act.wait_ge(first_landed, 48)
            act.wait_ge(dve_const, 1)
            with act.Fori(0, ITERS) as i:
                for step in STEPS:
                    kind, u, b, g = step
                    part, s = divmod(u, SETS)
                    if MISC.get(kind) == "act":
                        act.wait_ge(misc_ready, reached(i, N_MISC, BEFORE[step][3]))
                        bank = misc_ps[BEFORE[step][0]]
                    if kind == "raw_tr":
                        act.activation(xT[s][:, :], bank[:, 0:TOK], ACT.Copy)
                        act.activation(cT[s][:, :], bank[:, TOK:2 * TOK], ACT.Copy).then_inc(evac["act"], 1)
                    if kind == "ln_tr":
                        act.activation(hT[:, :], bank[:, 0:TOK], ACT.Identity,
                                       scale=col[:, C_AT["ln1_w"]:C_AT["ln1_w"] + 1],
                                       bias=col[:, C_AT["ln1_b"]:C_AT["ln1_b"] + 1])
                        act.activation(cnT[:, :], bank[:, TOK:2 * TOK], ACT.Identity,
                                       scale=col[:, C_AT["ln2_w"]:C_AT["ln2_w"] + 1],
                                       bias=col[:, C_AT["ln2_b"]:C_AT["ln2_b"] + 1]).then_inc(evac["act"], 1)
                    if kind == "qk":
                        scale = float(D // HEADS[part]) ** -0.5
                        act.wait_ge(split_done, reached(i, UNITS, u - 1))
                        if part <= L2:
                            bk = C_AT[f"bk{part}"]
                            act.activation(qk_f32[:, 0, :], bank[:, 0:TOK], ACT.Identity, scale=scale,
                                           bias=bq_scaled[:, part:part + 1])
                            act.activation(qk_f32[:, 1, :], bank[:, TOK:2 * TOK], ACT.Identity,
                                           bias=col[:, bk:bk + 1]).then_inc(evac["act"], 1)
                        else:
                            act.activation(qk_f32[:, 0, :], bank[:, 0:TOK], ACT.Copy, scale=scale)
                            act.activation(qk_f32[:, 1, :], bank[:, TOK:2 * TOK], ACT.Copy)\
                                .then_inc(evac["act"], 1)
                    if kind == "w1":
                        for half in range(2):
                            c = 2 * b + half
                            at = C_AT[f"m1_{part}_{c}"]
                            last = act.activation(hidden[:, c, :], bank[:, half * TOK:(half + 1) * TOK],
                                                  ACT.Gelu_apprx_tanh if part == L2 else ACT.Gelu,
                                                  bias=col[:, at:at + 1])
                        last.then_inc(evac["act"], 1)
                    if kind == "attn":
                        n = NUM[step]
                        act.wait_ge(attn_ready, reached(i, N_SCORE, n))
                        act.wait_ge(pv_done, reached(i, N_SCORE, n - 3))
                        src = attn_ps[n % 2][:, :].rearrange("p (h q) -> p h q", h=4)
                        if part == L1 and b == 0 and g == 0:
                            act.wait_ge(masks_ready, reached(i, 3, 2))
                        if part == L1:
                            bias = bias_l1[:, s * PAIR + b:s * PAIR + b + 1]
                            act.activation(probs[n % 3][:, :, :], src, ACT.Exp, bias=bias).then_inc(exp_done, 1)
                        elif part == L3C:
                            act.activation(probs[n % 3][:, :, :], src, ACT.Exp, bias=pad_bias[:, 0:1])\
                                .then_inc(exp_done, 1)
                        else:
                            act.activation(probs[n % 3][:, :, :], src, ACT.Exp).then_inc(exp_done, 1)
                    if kind == "o_evac":
                        n = ub(step)
                        cols_used = HEADS[part] // 4 * P
                        last_pv = the("pv", u, b, HEADS[part] // 4 - 1)
                        act.wait_ge(pv_done, reached(i, N_SCORE, NUM[last_pv]))
                        if n >= 2:
                            evacuated(act, i, the("o_tr", (n - 2) // PAIR, n % PAIR))
                        else:
                            evacuated(act, i, the("o_tr", UNITS - 1, n % PAIR), earlier=True)
                        act.activation(o_sb[n % 2][:, 0:cols_used], o_ps[n % 2][:, 0:cols_used], ACT.Copy)\
                            .then_inc(o_saved, 1)

        @block.vector
        def _(dve):
            for s_, per in ((evac["dve"], COUNT["dve"]), (score_reduced, N_SCORE), (term1_done, N_UB),
                            (maxrest_done, N_UB), (term2_done, N_UB), (maxterms_ready, N_UB),
                            (recip_done, N_UB), (stats_done, N_LN), (var_ready, N_LN), (input_normed, SETS),
                            (split1_done, UNITS)):
                dve.sem_inc(s_, per)
            for r in range(RING):
                dve.memset(v8[r][:, :], 1.0)
                dve.memset(v16[r][:, :], 1.0)
            for r in range(2):
                dve.memset(max_terms[r][:, :], 0.0)
            dve.wait_ge(first_landed, 48)
            for part in (L0, L1, L2):
                at = C_AT[f"bq{part}"]
                last = dve.tensor_scalar(bq_scaled[:, part:part + 1], col[:, at:at + 1],
                                         float(D // HEADS[part]) ** -0.5, None, ALU.mult)
            last.then_inc(dve_const, 1)
            with dve.Fori(0, ITERS) as i:
                for step in STEPS:
                    kind, u, b, g = step
                    part, s = divmod(u, SETS)
                    heads = HEADS[part]
                    d = D // heads
                    if MISC.get(kind) == "dve":
                        dve.wait_ge(misc_ready, reached(i, N_MISC, BEFORE[step][3]))
                        bank = misc_ps[BEFORE[step][0]]
                    if step in LN_STEPS:
                        n = LN_STEPS.index(step)
                        if kind == "ln_in":
                            dve.wait_ge(tokens_landed[s], 32 * (i + 1))
                            srcs = [t[s][:, k, :] for t in (x_tok, c_tok) for k in range(PAIR)]
                            dst = normed_in
                        else:
                            srcs = [bank[:, k * D:(k + 1) * D] for k in range(PAIR)]
                            dst = normed
                        for k, src in enumerate(srcs):
                            last = dve.bn_stats(stats[:, k, :], src)
                        last.then_inc(stats_done, 1)
                        dve.wait_ge(stats_done, reached(i, N_LN, n))
                        alone(dve)
                        for k in range(len(srcs)):
                            last = dve.bn_aggr(mean_var[:, k, :], stats[:, k, :])
                        last.then_inc(var_ready, 1)
                        dve.wait_ge(rstd_ready, reached(i, N_LN, n))
                        if kind == "ln_in":
                            if s:
                                evacuated(dve, i, the("ln_tr", s - 1))
                            else:
                                evacuated(dve, i, the("ln_tr", SETS - 1), earlier=True)
                        elif b == 1 and s:
                            dve.wait_ge(y_ready, reached(i, SETS, s - 1))
                        for k, src in enumerate(srcs):
                            last = dve.tensor_scalar(dst[:, k, :], src, mean_var[:, k, 0:1], rstd[:, k:k + 1],
                                                     ALU.subtract, ALU.mult)
                        last.then_inc(input_normed if kind == "ln_in" else evac["dve"], 1)
                    if kind == "split":
                        stacked(dve, i, u - 2)
                        alone(dve)
                        evacuated(dve, i, the("qk", u))
                        terms = terms_ring[u % 2]
                        dve.tensor_copy(terms[:, :, 0, :], qk_f32[:, :, :]).then_inc(split1_done, 1)
                    if kind == "v":
                        width = PAIR * heads * (d + 1)
                        dst = v_of(u)[:, 0:width].rearrange("p (n e) -> p n e", e=d + 1)[:, :, 0:d]
                        src = bank[:, 0:TOK].rearrange("p (n e) -> p n e", e=d)
                        if part <= L2:
                            for k in range(PAIR):
                                bias = row[:, R_AT[f"bv{part}"], :].rearrange("p (n e) -> p n e", e=d)
                                last = dve.tensor_tensor(dst[:, k * heads:(k + 1) * heads, :],
                                                         src[:, k * heads:(k + 1) * heads, :], bias, ALU.add)
                        else:
                            last = dve.tensor_copy(dst, src)
                        last.then_inc(evac["dve"], 1)
                    if kind == "score":
                        n = NUM[step]
                        dve.wait_ge(score_ready, reached(i, N_SCORE, n))
                        dve.tensor_reduce(negmax[ub(step) % 2][:, 4 * g:4 * g + 4],
                                          score_ps[n % 2][:, :].rearrange("p (h k) -> p h k", h=4),
                                          AX_X, ALU.max, negate=True).then_inc(score_reduced, 1)
                    if kind == "nmax":
                        n = ub(step)
                        nm, rm = negmax[n % 2][:, 0:heads], negmax_rest[n % 2][:, 0:heads]
                        mt = max_terms[n % 2]
                        dve.wait_ge(score_reduced, reached(i, N_SCORE, NUM[the("score", u, b, heads // 4 - 1)]))
                        dve.tensor_copy(mt[:, 0:heads], nm).then_inc(term1_done, 1)
                        dve.wait_ge(term1_done, reached(i, N_UB, n))
                        dve.tensor_tensor(rm, nm, mt[:, 0:heads], ALU.subtract).then_inc(maxrest_done, 1)
                        dve.wait_ge(maxrest_done, reached(i, N_UB, n))
                        dve.tensor_copy(mt[:, heads:2 * heads], rm).then_inc(term2_done, 1)
                        dve.wait_ge(term2_done, reached(i, N_UB, n))
                        dve.tensor_tensor(mt[:, 2 * heads:3 * heads], rm, mt[:, heads:2 * heads], ALU.subtract)\
                            .then_inc(maxterms_ready, 1)
                    if kind == "n_tr":
                        dve.tensor_copy(max_rows[ub(step) % 4][0:TERMS * heads, :],
                                        bank[0:TERMS * heads, 0:S // 2].bitcast(BF16)).then_inc(evac["dve"], 1)
                    if kind == "o_tr":
                        heads_ps = bank[:, 0:32 * heads].rearrange("p (h e) -> p h e", e=32)
                        dve.reciprocal(recip[:, 0:heads], heads_ps[:, :, d]).then_inc(recip_done, 1)
                        dve.wait_ge(recip_done, reached(i, N_UB, ub(step)))
                        dst = attn_tok[:, b, :].rearrange("p (h e) -> p h e", e=d)
                        spread = recip[:, 0:heads].unsqueeze(2).to_broadcast([P, heads, d])
                        if part == L1:
                            at = s * PAIR + b
                            dve.scalar_tensor_tensor(dst, heads_ps[:, :, 0:d], keep_l1[:, at:at + 1], spread,
                                                     ALU.mult, ALU.mult).then_inc(evac["dve"], 1)
                        else:
                            dve.tensor_tensor(dst, heads_ps[:, :, 0:d], spread, ALU.mult).then_inc(evac["dve"], 1)
                    if kind == "a_tr":
                        if part <= L1:
                            dve.tensor_tensor(xT[s][:, :], bank[:, 0:TOK], xT[s][:, :], ALU.add)\
                                .then_inc(evac["dve"], 1)
                        else:
                            dve.tensor_copy(attnT[:, :], bank[:, 0:TOK]).then_inc(evac["dve"], 1)
                    if kind in ("wo", "w2"):
                        at = C_AT[f"bo{part}" if kind == "wo" else f"m2_{part}"]
                        dve.scalar_tensor_tensor(xT[s][:, :], bank[:, 0:TOK], col[:, at:at + 1], xT[s][:, :],
                                                 ALU.add, ALU.add).then_inc(evac["dve"], 1)
                    if kind == "x_back":
                        dve.tensor_scalar(xT[s][:, :], bank[:, 0:TOK], col[:, C_AT[f"g{part}"]:C_AT[f"g{part}"] + 1],
                                          col[:, C_AT[f"b{part}"]:C_AT[f"b{part}"] + 1], ALU.mult, ALU.add)\
                            .then_inc(evac["dve"], 1)

        @block.tensor
        def _(pe):
            for s_, per in ((misc_ready, N_MISC), (score_ready, N_SCORE), (attn_ready, N_SCORE),
                            (pv_done, N_SCORE)):
                pe.sem_inc(s_, per)
            pe.wait_ge(pool_const, 10)
            pe.wait_ge(fill_landed, 16 * 3 * RING)
            pe.wait_ge(first_landed, 48)

            def weight(name):
                return w[:, W_AT[name], :]

            with pe.Fori(0, ITERS) as i:
                for step in STEPS:
                    kind, u, b, g = step
                    part, s = divmod(u, SETS)
                    heads = HEADS[part]
                    d = D // heads
                    pairs = stack_of(u)
                    if kind in MISC:
                        n_bank, held, same, _n = BEFORE[step]
                        evacuated(pe, i, held, earlier=not same)
                        bank = misc_ps[n_bank]
                    if kind in ("qk", "x_tr", "w1"):
                        wrote = x_written_before(step)
                        if wrote is not None:
                            evacuated(pe, i, wrote)
                    if kind == "raw_tr":
                        pe.wait_ge(tokens_landed[s], 32 * (i + 1))
                        for k, src in enumerate([t[s][:, j, :] for t in (x_tok, c_tok) for j in range(PAIR)]):
                            last = pe.transpose(bank[:, k * P:(k + 1) * P], src, ident[:, :])
                        last.then_inc(misc_ready, 1)
                    if kind == "ln_tr":
                        pe.wait_ge(input_normed, reached(i, SETS, s))
                        for k in range(2 * PAIR):
                            last = pe.transpose(bank[:, k * P:(k + 1) * P], normed_in[:, k, :], ident[:, :])
                        last.then_inc(misc_ready, 1)
                    if kind == "qk":
                        if part == L0:
                            evacuated(pe, i, the("ln_tr", u))
                        if u == SETS:
                            pe.wait_ge(weights_landed, 16)
                        qsrc = hT if part == L0 else xT[s]
                        ksrc = cnT if part == L0 else xT[s] if part == L3S else cT[s]
                        pe.matmul(bank[:, 0:TOK], weight(f"q{part}"), qsrc[:, :], start=True, stop=True)
                        pe.matmul(bank[:, TOK:2 * TOK], weight(f"k{part}"), ksrc[:, :], start=True, stop=True)\
                            .then_inc(misc_ready, 1)
                    if kind == "v":
                        vsrc = cnT if part == L0 else xT[s] if part == L3S else cT[s]
                        for k in range(PAIR):
                            last = pe.matmul(bank[:, k * P:(k + 1) * P], vsrc[:, k * S:(k + 1) * S],
                                             weight(f"v{part}"), start=True, stop=True)
                        last.then_inc(misc_ready, 1)
                    if kind == "score":
                        n = NUM[step]
                        if b == 0 and g == 0:
                            stacked(pe, i, u)
                        if part == L1 and b == 0 and g == 0:
                            pe.wait_ge(masks_ready, reached(i, 3, 2))
                        pe.wait_ge(score_reduced, reached(i, N_SCORE, n - 2))
                        mask = {L1: mask_l1[:, s * PAIR + b, :], L3S: mask_l3[:, :], L3C: pad_neg[:, :]}.get(part)
                        if mask is not None:
                            pe.matmul(score_ps[n % 2][:, :], ident_bf[:, :],
                                      mask.unsqueeze(1).to_broadcast([P, 4, S]), start=True, stop=False,
                                      skip_group_check=True)
                        for j in range(4):
                            h = 4 * g + j
                            last = pe.matmul(score_ps[n % 2][:, j * S:(j + 1) * S],
                                             pairs[0:STACK, h, 0, b * S:(b + 1) * S],
                                             pairs[0:STACK, h, 1, b * S:(b + 1) * S],
                                             start=mask is None, stop=True, skip_group_check=True)
                        last.then_inc(score_ready, 1)
                    if kind == "n_tr":
                        m = ub(step)
                        pe.wait_ge(maxterms_ready, reached(i, N_UB, m))
                        pe.transpose(bank[:, 0:S // 2].bitcast(BF16), max_terms[m % 2][:, :], ident_bf[:, :])\
                            .then_inc(misc_ready, 1)
                    if kind == "attn":
                        n, m = NUM[step], ub(step)
                        if g == 0:
                            pe.wait_ge(max_landed[m % 2], reached(i, N_UB // 2, m // 2) * 16)
                        pe.wait_ge(exp_done, reached(i, N_SCORE, n - 2))
                        mask = {L1: causal_t, L3S: mask_l3_t}.get(part)
                        if mask is not None:
                            pe.matmul(attn_ps[n % 2][:, :], ident_bf[:, :],
                                      mask[:, :].unsqueeze(1).to_broadcast([P, 4, S]), start=True, stop=False,
                                      skip_group_check=True)
                        for j in range(4):
                            h = 4 * g + j
                            last = pe.matmul(attn_ps[n % 2][:, j * S:(j + 1) * S],
                                             pairs[0:ROWS, h, 1, b * S:(b + 1) * S],
                                             pairs[0:ROWS, h, 0, b * S:(b + 1) * S],
                                             start=mask is None, stop=True, skip_group_check=True)
                        last.then_inc(attn_ready, 1)
                    if kind == "pv":
                        n, m = NUM[step], ub(step)
                        pe.wait_ge(exp_done, reached(i, N_SCORE, n))
                        if g == 0:
                            pe.wait_ge(o_saved, reached(i, N_UB, m - 2))
                            evacuated(pe, i, the("v", u))
                        for j in range(4):
                            at = (b * heads + 4 * g + j) * (d + 1)
                            last = pe.matmul(o_ps[m % 2][32 * j:32 * j + 32, g * P:(g + 1) * P],
                                             v_of(u)[:, at:at + 32], probs[n % 3][:, j, :],
                                             start=True, stop=True, skip_group_check=True)
                        last.then_inc(pv_done, 1)
                    if kind == "o_tr":
                        pe.wait_ge(o_saved, reached(i, N_UB, ub(step)))
                        for k in range(heads // 4):
                            last = pe.transpose(bank[:, k * P:(k + 1) * P], o_sb[ub(step) % 2][:, k * P:(k + 1) * P],
                                                ident[:, :])
                        last.then_inc(misc_ready, 1)
                    if kind == "a_tr":
                        evacuated(pe, i, the("o_tr", u, 1))
                        for k in range(PAIR):
                            last = pe.transpose(bank[:, k * P:(k + 1) * P], attn_tok[:, k, :], ident[:, :])
                        last.then_inc(misc_ready, 1)
                    if kind == "wo":
                        evacuated(pe, i, the("a_tr", u))
                        pe.matmul(bank[:, 0:TOK], weight(f"o{part}"), attnT[:, :], start=True, stop=True)\
                            .then_inc(misc_ready, 1)
                    if kind == "w1":
                        for half in range(2):
                            last = pe.matmul(bank[:, half * TOK:(half + 1) * TOK], weight(f"w1_{part}_{2 * b + half}"),
                                             xT[s][:, :], start=True, stop=True)
                        last.then_inc(misc_ready, 1)
                    if kind == "w2":
                        evacuated(pe, i, the("w1", u, 1))
                        for c in range(4):
                            last = pe.matmul(bank[:, 0:TOK], weight(f"w2_{part}_{c}"), hidden[:, c, :],
                                             start=(c == 0), stop=(c == 3))
                        last.then_inc(misc_ready, 1)
                    if kind == "x_tr":
                        for k in range(PAIR):
                            last = pe.transpose(bank[:, k * P:(k + 1) * P], xT[s][:, k * S:(k + 1) * S], ident[:, :])
                        last.then_inc(misc_ready, 1)
                    if kind == "x_back":
                        evacuated(pe, i, the("x_tr", u, 0))
                        for k in range(PAIR):
                            last = pe.transpose(bank[:, k * P:(k + 1) * P], normed[:, k, :], ident[:, :])
                        last.then_inc(misc_ready, 1)


def kernel(**inputs):
    import numpy as np
    import concourse.bacc as bacc
    from concourse.bass_utils import run_bass_kernel_spmd

    a = {k: np.asarray(v) for k, v in inputs.items()}

    def by_channel(m, heads):
        return m.reshape(m.shape[:-1] + (heads, D // heads)).swapaxes(-1, -2).reshape(m.shape)

    qkv = np.split(a["L3_xattn_Wqkv"], 3, axis=1)
    mats = {"o2": a["L2_xattn_Wo"], "o3": a["L3_xattn_Wo1"], "o4": a["L3_xattn_Wo2"]}
    for part, (q, k, v) in enumerate((
            [a[f"L0_xattn_W{m}"].T for m in "qkv"], [a[f"L1_xattn_W{m}"].T for m in "qkv"],
            [a[f"L2_xattn_W{m}"] for m in "qkv"], qkv, [a[f"L3_xattn_W{m}"] for m in "qkv"])):
        mats |= {f"q{part}": by_channel(q, HEADS[part]), f"k{part}": by_channel(k, HEADS[part]), f"v{part}": v}
    for part, layer in ((L2, "L2"), (L3C, "L3")):
        for c in range(4):
            mats[f"w1_{part}_{c}"] = a[f"{layer}_xattn_W1"][:, c * P:(c + 1) * P]
            mats[f"w2_{part}_{c}"] = a[f"{layer}_xattn_W2"][c * P:(c + 1) * P]
    vecs = {"ln1_w": "L0_xattn_ln1_w", "ln1_b": "L0_xattn_ln1_b", "ln2_w": "L0_xattn_ln2_w", "ln2_b": "L0_xattn_ln2_b",
            "bo2": "L2_xattn_bo", "bo3": "L3_xattn_bo1", "bo4": "L3_xattn_bo2", "m2_2": "L2_xattn_b2",
            "m2_4": "L3_xattn_bf2", "g3": "L3_xattn_g1", "b3": "L3_xattn_b1", "g4": "L3_xattn_g2",
            "b4": "L3_xattn_b2"}
    vecs = {n: a[v] for n, v in vecs.items()}
    for part in (L0, L1, L2):
        for m in "qk":
            vecs[f"b{m}{part}"] = by_channel(a[f"L{part}_xattn_b{m}"], HEADS[part])
    for c in range(4):
        vecs[f"m1_{L2}_{c}"] = a["L2_xattn_b1"][c * P:(c + 1) * P]
        vecs[f"m1_{L3C}_{c}"] = a["L3_xattn_bf1"][c * P:(c + 1) * P]
    bcast = {"bv0": a["L0_xattn_bv"], "bv1": a["L1_xattn_bv"], "bv2": a["L2_xattn_bv"],
             "g5": a["L3_xattn_g3"], "b5": a["L3_xattn_b3"]}
    valid, pad = a["mask_BxS2_bk1"], a["mask_1xS2_if1"]
    arrays = {
        "x": a["x"], "ctx": a["ctx_1024"],
        "weights": np.stack([mats[n] for n in W_NAMES], axis=1),
        "cols": np.stack([vecs[n] for n in C_NAMES], axis=1),
        "rows": np.stack([bcast[n] for n in R_NAMES]),
        "valid": valid, "valid_t": valid.T, "pad": pad[0], "pad_t": pad.T,
    }
    arrays = {f"in_{n}_dram": np.ascontiguousarray(v) for n, v in arrays.items()}
    nc = bacc.Bacc("TRN2", target_bir_lowering=False, num_devices=1)
    args = [nc.dram_tensor(n, v.shape, mybir.dt.from_np(v.dtype), kind="ExternalInput").ap()
            for n, v in arrays.items()]
    args.append(nc.dram_tensor("out_dram", (BATCHES, S, D), F32, kind="ExternalOutput").ap())
    build(nc, *args)
    result = run_bass_kernel_spmd(nc, [arrays], core_ids=[0])
    return result.results[0]["out_dram"]
```

```python
from collections import namedtuple
from contextlib import ExitStack

import concourse.bass as bass
from concourse import mybir

F32 = mybir.dt.float32
BF16 = mybir.dt.bfloat16
U32 = mybir.dt.uint32
I32 = mybir.dt.int32
U8 = mybir.dt.uint8
ALU = mybir.AluOpType
ACT = mybir.ActivationFunctionType
AX_X = mybir.AxisListType.X

P = 128
BATCHES, S, D, FF = 16, 128, 128, 512
PAIR = 2
SETS = BATCHES // PAIR
TOK = PAIR * S
PARTS = 5
L0, L1, L2, L3S, L3C = range(PARTS)
HEADS = (8, 16, 16, 16, 16)
UNITS = PARTS * SETS
STACK = 96
TERMS = 3
ROWS = STACK + TERMS
PRODUCTS = ((0, 0), (0, 1), (1, 0), (0, 2), (2, 0), (1, 1))
BIG = float(2 ** 100)
RING = 3
LN_RING = 4
MISC_BANKS = 3
SLOT = 8
EPS_LN, EPS_LAST = 1e-5, 1e-6

W_NAMES = ([f"{m}{p}" for p in range(PARTS) for m in "qkv"] + ["o2", "o3", "o4"]
           + [f"w1_{l}_{c}" for l in (2, 4) for c in range(4)] + [f"w2_{l}_{c}" for l in (2, 4) for c in range(4)])
W_AT = {n: i for i, n in enumerate(W_NAMES)}
W_FIRST = 3
C_NAMES = ["ln1_w", "ln1_b", "ln2_w", "ln2_b", "bq0", "bk0", "bq1", "bk1", "bq2", "bk2", "bo2", "bo3", "bo4",
           "m2_2", "m2_4", "g3", "b3", "g4", "b4"] + [f"m1_{l}_{c}" for l in (2, 4) for c in range(4)]
C_AT = {n: i for i, n in enumerate(C_NAMES)}
R_NAMES = ["bv0", "bv1", "bv2", "g5", "b5"]
R_AT = {n: i for i, n in enumerate(R_NAMES)}

BEFORE_ATTENDING = {
    L0: (("load", -44), ("ln_in", -32), ("raw_tr", -30), ("ln_norm", -27), ("ln_tr", -25), ("qk", -20), ("split", -20),
         ("v", -15), ("mask", -14)),
    "others": (("qk", -20), ("split", -20), ("v", -15)),
}
STACK_AT = -16
CHAIN = {
    L0: ((10, "a_tr"),),
    L1: ((10, "a_tr"),),
    L2: ((10, "a_tr"), (12, "wo"), (14, "w1"), (14, "w1"), (17, "w2")),
    L3S: ((10, "a_tr"), (12, "wo"), (14, "x_tr"), (15, "x_stats"), (17, "x_norm"), (19, "x_back")),
    L3C: ((10, "a_tr"), (12, "wo"), (14, "x_tr"), (15, "x_stats"), (17, "x_norm"), (19, "x_back"), (21, "w1"), (21, "w1"), (24, "w2"),
          (27, "x_tr"), (28, "x_stats"), (30, "x_norm"), (31, "out")),
}

Step = namedtuple("Step", "kind u b g")
MISC = {"raw_tr": "act", "ln_tr": "act", "qk": "act", "v": "dve", "n_tr": "dve", "o_tr": "dve", "a_tr": "dve",
        "wo": "dve", "w1": "act", "w2": "dve", "x_tr": "act", "x_back": "dve"}


def schedule():
    at = {}

    def put(slot, pos, rank, step):
        at.setdefault((slot * SLOT + pos, rank, len(at)), step)

    for u in range(UNITS):
        part = u // SETS
        banks = HEADS[part] // 4
        every = 4 // banks
        for kind, pos in BEFORE_ATTENDING.get(part, BEFORE_ATTENDING["others"]):
            put(u, pos, 2, Step(kind, u, 0, 0))
        for c in range(len(PRODUCTS)):
            put(u, STACK_AT + c // 2, 2, Step("stack", u, c, 0))
        for b in range(PAIR):
            for g in range(banks):
                pos = 4 * b + every * g
                put(u - 1, pos, 1, Step("score", u, b, g))
                put(u, pos, 0, Step("attn", u, b, g))
                put(u, pos + 1, 0.5, Step("pv", u, b, g))
            last = 4 * b + every * (banks - 1)
            put(u - 1, last, 1.1, Step("nmax", u, b, 0))
            put(u - 1, last + 2, 1.5, Step("n_tr", u, b, 0))
            put(u, last + 1, 0.6, Step("o_evac", u, b, 0))
            put(u, last + 2, 1.6, Step("o_tr", u, b, 0))
        seen = {}
        for pos, kind in CHAIN[part]:
            seen[kind] = seen.get(kind, -1) + 1
            put(u, pos, 3, Step(kind, u, seen[kind], 0))
    return [at[k] for k in sorted(at)]


STEPS = schedule()


def numbering():
    count, num, evac, order, before = {}, {}, {}, {}, {}
    last = [None] * MISC_BANKS
    for n, s in enumerate([s for s in STEPS if s.kind in MISC]):
        e = MISC[s.kind]
        evac[s] = count.get(e, 0)
        count[e] = evac[s] + 1
        order[s], before[s] = n, last[n % MISC_BANKS]
        last[n % MISC_BANKS] = s
    for s in STEPS:
        num[s] = count.get(s.kind, 0)
        count[s.kind] = num[s] + 1
    return num, evac, order, before


NUM, EVAC, ORDER, BEFORE = numbering()
X_WRITES = [s for s in STEPS if s.kind in ("wo", "w2", "x_back") or (s.kind == "a_tr" and s.u // SETS <= L1)]
LN_STEPS = [s for s in STEPS if s.kind in ("ln_in", "x_stats")]
NORM_STEPS = [s for s in STEPS if s.kind == "x_norm"]


def x_written_before(step):
    found = None
    for s in STEPS[:STEPS.index(step)]:
        if s in X_WRITES and s.u % SETS == step.u % SETS:
            found = s
    return found


def build(nc, x, ctx_in, weights, cols, rows, valid, valid_t, pad, pad_t, out):
    with ExitStack() as stack:
        def sb(name, shape, dt=F32):
            return stack.enter_context(nc.sbuf_tensor(name, shape, dt))

        def sem(name):
            return stack.enter_context(nc.semaphore(name))

        w = sb("w", [P, len(W_NAMES), P])
        col = sb("col", [P, len(C_NAMES)])
        bq_scaled = sb("bq_scaled", [P, 3])
        row = sb("row", [P, len(R_NAMES), P])
        ident = sb("ident", [P, P])
        ident_bf = sb("ident_bf", [P, P], BF16)
        causal_t = sb("causal_t", [P, S], BF16)
        valid_raw = sb("valid_raw", [P, BATCHES, S], U8)
        valid_neg = sb("valid_neg", [P, BATCHES, S], BF16)
        mask_l1 = sb("mask_l1", [P, BATCHES, S], BF16)
        validt_raw = sb("validt_raw", [P, BATCHES], U8)
        keep_l1 = sb("keep_l1", [P, BATCHES])
        bias_l1 = sb("bias_l1", [P, BATCHES])
        pad_raw = sb("pad_raw", [P, S], I32)
        padt_raw = sb("padt_raw", [P, 1], I32)
        pad_neg = sb("pad_neg", [P, S], BF16)
        pad_bias = sb("pad_bias", [P, 1])
        mask_l3 = sb("mask_l3", [P, S], BF16)
        mask_l3_t = sb("mask_l3_t", [P, S], BF16)
        one_rows = sb("one_rows", [P, TOK], BF16)
        zero_rows = sb("zero_rows", [STACK // 2, 2 * TOK], BF16)
        minus_half = sb("minus_half", [P, 4])

        x_tok = [sb(f"x_tok{s}", [P, PAIR, D]) for s in range(SETS)]
        c_tok = [sb(f"c_tok{s}", [P, PAIR, D]) for s in range(SETS)]
        xT = [sb(f"xT{s}", [P, TOK]) for s in range(SETS)]
        cT = [sb(f"cT{s}", [P, TOK]) for s in range(SETS)]
        y = x_tok
        hT = [sb(f"hT{r}", [P, TOK]) for r in range(2)]
        cnT = [sb(f"cnT{r}", [P, TOK]) for r in range(2)]
        stats = sb("stats", [P, 2 * PAIR, 6])
        mean_var_ring = [sb(f"mean_var{r}", [P, 2 * PAIR, 2]) for r in range(LN_RING)]
        var_eps = sb("var_eps", [P, 2 * PAIR])
        rstd_ring = [sb(f"rstd{r}", [P, 2 * PAIR]) for r in range(LN_RING)]
        normed_in_ring = [sb(f"normed_in{r}", [P, 2 * PAIR, D]) for r in range(2)]
        x_rows = [sb(f"x_rows{r}", [P, TOK]) for r in range(2)]
        normed_ring = [sb(f"normed{r}", [P, PAIR, D]) for r in range(2)]
        qk_f32 = sb("qk_f32", [P, 2, TOK])
        rest = sb("rest", [P, 2, TOK])
        terms_ring = [sb(f"terms{r}", [P, 2, TERMS, TOK], BF16) for r in range(2)]
        pairs8 = [sb(f"pairs8_{r}", [P, 8, 2, TOK], BF16) for r in range(RING)]
        pairs16 = [sb(f"pairs16_{r}", [P, 16, 2, TOK], BF16) for r in range(RING)]
        v8 = [sb(f"v8_{r}", [P, PAIR * 8 * 17 + 16]) for r in range(RING)]
        v16 = [sb(f"v16_{r}", [P, PAIR * 16 * 9 + 24]) for r in range(RING)]
        negmax = [sb(f"negmax{r}", [P, 16]) for r in range(2)]
        negmax_rest = [sb(f"negmax_rest{r}", [P, 16]) for r in range(2)]
        max_terms = [sb(f"max_terms{r}", [P, P], BF16) for r in range(2)]
        max_rows = [sb(f"max_rows{r}", [TERMS * 16, S], BF16) for r in range(4)]
        probs = [sb(f"probs{r}", [P, 4, S]) for r in range(3)]
        o_sb = [sb(f"o_sb{r}", [P, 512]) for r in range(2)]
        recip = sb("recip", [P, 16])
        attn_tok = sb("attn_tok", [P, PAIR, D])
        attnT = sb("attnT", [P, TOK])
        hidden = sb("hidden", [P, 4, TOK])

        score_ps = [stack.enter_context(nc.psum_tensor(f"score_ps{r}", [P, 512], F32)) for r in range(2)]
        attn_ps = [stack.enter_context(nc.psum_tensor(f"attn_ps{r}", [P, 512], F32)) for r in range(2)]
        o_ps = stack.enter_context(nc.psum_tensor("o_ps", [P, 512], F32))
        misc_ps = [stack.enter_context(nc.psum_tensor(f"misc_ps{r}", [P, 512], F32)) for r in range(MISC_BANKS)]

        first_landed = sem("first_landed")
        weights_landed = sem("weights_landed")
        masks_landed = sem("masks_landed")
        tokens_landed = [sem(f"tokens_landed{s}") for s in range(SETS)]
        valid_landed = sem("valid_landed")
        stack_landed = [sem(f"stack_landed{r}") for r in range(RING)]
        max_landed = [sem(f"max_landed{r}") for r in range(2)]
        out_landed = sem("out_landed")
        pool_const = sem("pool_const")
        dve_const = sem("dve_const")
        bias_l1_ready = sem("bias_l1_ready")
        negated = sem("negated")
        mask_l1_ready = sem("mask_l1_ready")
        fill8_landed = sem("fill8_landed")
        fill16_landed = sem("fill16_landed")
        pool_mask = sem("pool_mask")
        misc_ready = sem("misc_ready")
        evac = {"act": sem("evac_act"), "dve": sem("evac_dve")}
        score_ready = sem("score_ready")
        score_reduced = sem("score_reduced")
        term1_done = sem("term1_done")
        maxrest_done = sem("maxrest_done")
        term2_done = sem("term2_done")
        maxterms_ready = sem("maxterms_ready")
        attn_ready = sem("attn_ready")
        exp_done = sem("exp_done")
        pv_done = sem("pv_done")
        o_saved = sem("o_saved")
        recip_done = sem("recip_done")
        stats_done = sem("stats_done")
        var_ready = sem("var_ready")
        eps_added = sem("eps_added")
        rstd_ready = sem("rstd_ready")
        input_normed = sem("input_normed")
        split1_done = sem("split1_done")
        split2_done = sem("split2_done")
        split_done = sem("split_done")
        scaled_g = sem("scaled_g")
        x_normed = sem("x_normed")
        y_ready = sem("y_ready")

        def evacuated(eng, step):
            eng.wait_ge(evac[MISC[step.kind]], EVAC[step] + 1)

        def ub(s):
            return s.u * PAIR + s.b

        def stack_of(u):
            return (pairs8 if u // SETS == L0 else pairs16)[u % RING]

        def v_of(u):
            return (v8 if u // SETS == L0 else v16)[u % RING]

        def stacked(eng, u):
            eng.wait_ge(stack_landed[u % RING], (u // RING + 1) * 16 * len(PRODUCTS))

        def the(kind, u, b=0, g=0):
            return Step(kind, u, b, g)

        block = stack.enter_context(nc.Block())

        @block.sync
        def _(sp):
            for step in STEPS:
                u = step.u
                heads = HEADS[u // SETS]
                if step.kind == "load":
                    first = u * PAIR
                    sp.dma_start(x_tok[u][:, :, :], x[first:first + PAIR].rearrange("b t d -> t b d"))\
                        .then_inc(tokens_landed[u], 16)
                    sp.dma_start(c_tok[u][:, :, :], ctx_in[first:first + PAIR].rearrange("b t d -> t b d"))\
                        .then_inc(tokens_landed[u], 16)
                    if u == 0:
                        sp.dma_start(w[:, 0:W_FIRST, :], weights[:, 0:W_FIRST, :]).then_inc(first_landed, 16)
                        sp.dma_start(col[:, :], cols).then_inc(first_landed, 16)
                        sp.dma_start(row[:, :, :], rows.partition_broadcast(P)).then_inc(first_landed, 16)
                if step.kind == "stack":
                    c = step.b
                    if c == 0:
                        sp.wait_ge(split_done, u + 1)
                        if u >= RING:
                            sp.wait_ge(o_saved, (u - RING + 1) * PAIR)
                    d = D // heads
                    tq, tk = PRODUCTS[c]
                    terms = terms_ring[u % 2]
                    gap = TERMS + tk - tq
                    sp.dma_start(stack_of(u)[c * d:(c + 1) * d, :, :, :],
                                 terms[:, :, :, :].rearrange("p a t n -> p (a t) n")[:, tq:tq + gap + 1:gap, :])\
                        .then_inc(stack_landed[u % RING], 16)
                if step.kind == "n_tr":
                    evacuated(sp, step)
                    n = ub(step)
                    sp.dma_start(stack_of(u)[STACK:ROWS, :, 0, step.b * S:(step.b + 1) * S],
                                 max_rows[n % 4][0:TERMS * heads, :]).then_inc(max_landed[n % 2], 16)

        @block.gpsimd
        def _(pool):
            pool.dma_start(padt_raw[:, :], pad_t).then_inc(masks_landed, 16)
            pool.dma_start(pad_raw[:, :], pad.partition_broadcast(P)).then_inc(masks_landed, 16)
            pool.dma_start(validt_raw[:, :], valid_t).then_inc(masks_landed, 16)
            pool.dma_start(w[:, W_FIRST:, :], weights[:, W_FIRST:, :]).then_inc(weights_landed, 16)
            pool.memset(one_rows[:, :], 1.0).then_inc(pool_const, 1)
            pool.memset(zero_rows[:, :], 0.0).then_inc(pool_const, 1)
            pool.memset(ident[:, :], 0.0).then_inc(pool_const, 1)
            pool.memset(causal_t[:, :], 0.0).then_inc(pool_const, 1)
            pool.memset(minus_half[:, :], -0.5).then_inc(pool_const, 1)
            pool.wait_ge(pool_const, 5)
            pool.affine_select(out=ident[:, :], in_=ident[:, :], compare_op=ALU.not_equal, fill=1.0, base=0,
                               pattern=[[-1, P]], channel_multiplier=1).then_inc(pool_const, 1)
            pool.affine_select(out=causal_t[:, :], in_=causal_t[:, :], compare_op=ALU.is_ge, fill=-BIG, base=0,
                               pattern=[[1, S]], channel_multiplier=-1).then_inc(pool_const, 1)
            pool.wait_ge(pool_const, 7)
            pool.tensor_copy(ident_bf[:, :], ident[:, :]).then_inc(pool_const, 1)
            pool.wait_ge(masks_landed, 48)
            pool.tensor_scalar(pad_neg[:, :], pad_raw[:, :], 1.0, BIG, ALU.subtract, ALU.mult).then_inc(pool_mask, 1)
            pool.tensor_scalar(pad_bias[:, :], padt_raw[:, :], 1.0, BIG, ALU.subtract, ALU.mult)\
                .then_inc(pool_mask, 1)
            pool.tensor_copy(keep_l1[:, :], validt_raw[:, :]).then_inc(pool_mask, 1)
            pool.wait_ge(pool_mask, 3)
            pool.affine_select(out=mask_l3[:, :], in_=pad_neg[:, :], compare_op=ALU.is_ge, fill=-BIG, base=0,
                               pattern=[[-1, S]], channel_multiplier=1).then_inc(pool_const, 1)
            pool.tensor_scalar(mask_l3_t[:, :], causal_t[:, :], pad_bias[:, 0:1], None, ALU.min)\
                .then_inc(pool_const, 1)
            pool.dma_start(valid_raw[:, :, :], valid.partition_broadcast(P))\
                .then_inc(valid_landed, 16)
            pool.tensor_scalar(bias_l1[:, :], keep_l1[:, :], 1.0, BIG, ALU.subtract, ALU.mult)\
                .then_inc(bias_l1_ready, 1)
            for step in STEPS:
                u = step.u
                if step.kind == "mask":
                    two = slice(PAIR * u, PAIR * (u + 1))
                    if u == 0:
                        pool.wait_ge(valid_landed, 16)
                    pool.tensor_scalar(valid_neg[:, two, :], valid_raw[:, two, :], 1.0, BIG, ALU.subtract, ALU.mult)\
                        .then_inc(negated, 1)
                    pool.wait_ge(negated, u + 1)
                    pool.affine_select(out=mask_l1[:, two, :], in_=valid_neg[:, two, :], compare_op=ALU.is_ge,
                                       fill=-BIG, base=0, pattern=[[0, PAIR], [-1, S]],
                                       channel_multiplier=1).then_inc(mask_l1_ready, 1)
                if step in LN_STEPS:
                    n = LN_STEPS.index(step)
                    k = 2 * PAIR if step.kind == "ln_in" else PAIR
                    eps = EPS_LAST if step.kind == "x_stats" and step.b == 1 else EPS_LN
                    pool.wait_ge(var_ready, n + 1)
                    pool.tensor_scalar(var_eps[:, 0:k], mean_var_ring[n % LN_RING][:, 0:k, 1], eps, None, ALU.add)\
                        .then_inc(eps_added, 1)
                    pool.wait_ge(eps_added, n + 1)
                    pool.tensor_tensor(rstd_ring[n % LN_RING][:, 0:k], var_eps[:, 0:k], minus_half[:, 0:k], ALU.pow)\
                        .then_inc(rstd_ready, 1)
                if step.kind == "split":
                    terms = terms_ring[u % 2]
                    pool.wait_ge(split1_done, u + 1)
                    pool.tensor_tensor(rest[:, :, :], qk_f32[:, :, :], terms[:, :, 0, :], ALU.subtract)
                    pool.tensor_tensor(terms[:, :, 1, :], qk_f32[:, :, :], terms[:, :, 0, :], ALU.subtract)\
                        .then_inc(split2_done, 1)
                    pool.wait_ge(split2_done, u + 1)
                    pool.tensor_tensor(terms[:, :, 2, :], rest[:, :, :], terms[:, :, 1, :], ALU.subtract)\
                        .then_inc(split_done, 1)
                if step.kind == "out":
                    s = u % SETS
                    pool.wait_ge(x_normed, NORM_STEPS.index(the("x_norm", u, 1)) + 1)
                    normed = normed_ring[NORM_STEPS.index(the("x_norm", u, 1)) % 2]
                    pool.tensor_tensor(y[s][:, :, :], normed[:, :, :],
                                       row[:, R_AT["g5"], :].unsqueeze(1).to_broadcast([P, PAIR, D]),
                                       ALU.mult).then_inc(scaled_g, 1)
                    pool.wait_ge(scaled_g, s + 1)
                    pool.tensor_tensor(y[s][:, :, :], y[s][:, :, :],
                                       row[:, R_AT["b5"], :].unsqueeze(1).to_broadcast([P, PAIR, D]),
                                       ALU.add).then_inc(y_ready, 1)
                    pool.wait_ge(y_ready, s + 1)
                    pool.dma_start(out[s * PAIR:(s + 1) * PAIR].rearrange("b t d -> t b d"),
                                   y[s][:, :, :]).then_inc(out_landed, 16)
            pool.wait_ge(out_landed, 16 * SETS)

        @block.scalar
        def _(act):
            act.wait_ge(pool_const, 2)
            for buffers, heads, landed in ((pairs8, 8, fill8_landed), (pairs16, 16, fill16_landed)):
                for pairs in buffers:
                    act.dma_start(pairs[STACK:ROWS, :, 1, :],
                                  one_rows[0:TERMS, :].unsqueeze(1).to_broadcast([TERMS, heads, TOK]))\
                        .then_inc(landed, 16)
            for pairs in pairs16:
                act.dma_start(pairs[STACK // 2:STACK, :, :, :].rearrange("p h a n -> p h (a n)"),
                              zero_rows[:, :].unsqueeze(1).to_broadcast([STACK // 2, 16, 2 * TOK]))\
                    .then_inc(fill16_landed, 16)
            act.wait_ge(first_landed, 48)
            act.wait_ge(dve_const, 1)
            for step in STEPS:
                kind, u, b, g = step
                part, s = divmod(u, SETS)
                if MISC.get(kind) == "act":
                    act.wait_ge(misc_ready, ORDER[step] + 1)
                    bank = misc_ps[ORDER[step] % MISC_BANKS]
                if kind == "raw_tr":
                    act.activation(xT[s][:, :], bank[:, 0:TOK], ACT.Copy)
                    act.activation(cT[s][:, :], bank[:, TOK:2 * TOK], ACT.Copy).then_inc(evac["act"], 1)
                if kind == "ln_tr":
                    if u >= 2:
                        evacuated(act, the("v", u - 2))
                    act.activation(hT[u % 2][:, :], bank[:, 0:TOK], ACT.Identity,
                                   scale=col[:, C_AT["ln1_w"]:C_AT["ln1_w"] + 1],
                                   bias=col[:, C_AT["ln1_b"]:C_AT["ln1_b"] + 1])
                    act.activation(cnT[u % 2][:, :], bank[:, TOK:2 * TOK], ACT.Identity,
                                   scale=col[:, C_AT["ln2_w"]:C_AT["ln2_w"] + 1],
                                   bias=col[:, C_AT["ln2_b"]:C_AT["ln2_b"] + 1]).then_inc(evac["act"], 1)
                if kind == "qk":
                    scale = float(D // HEADS[part]) ** -0.5
                    if u:
                        act.wait_ge(split_done, u)
                    if part <= L2:
                        bk = C_AT[f"bk{part}"]
                        act.activation(qk_f32[:, 0, :], bank[:, 0:TOK], ACT.Identity, scale=scale,
                                       bias=bq_scaled[:, part:part + 1])
                        act.activation(qk_f32[:, 1, :], bank[:, TOK:2 * TOK], ACT.Identity,
                                       bias=col[:, bk:bk + 1]).then_inc(evac["act"], 1)
                    else:
                        act.activation(qk_f32[:, 0, :], bank[:, 0:TOK], ACT.Copy, scale=scale)
                        act.activation(qk_f32[:, 1, :], bank[:, TOK:2 * TOK], ACT.Copy)\
                            .then_inc(evac["act"], 1)
                if kind == "x_tr":
                    m = NORM_STEPS.index(the("x_norm", u, b))
                    if m >= 2:
                        act.wait_ge(x_normed, m - 1)
                    act.activation(x_rows[m % 2][:, :], bank[:, 0:TOK], ACT.Copy).then_inc(evac["act"], 1)
                if kind == "w1":
                    for half in range(2):
                        c = 2 * b + half
                        at = C_AT[f"m1_{part}_{c}"]
                        last = act.activation(hidden[:, c, :], bank[:, half * TOK:(half + 1) * TOK],
                                              ACT.Gelu_apprx_tanh if part == L2 else ACT.Gelu,
                                              bias=col[:, at:at + 1])
                    last.then_inc(evac["act"], 1)
                if kind == "attn":
                    n = NUM[step]
                    act.wait_ge(attn_ready, n + 1)
                    if n >= 3:
                        act.wait_ge(pv_done, n - 2)
                    src = attn_ps[n % 2][:, :].rearrange("p (h q) -> p h q", h=4)
                    if part == L1 and b == 0 and g == 0:
                        act.wait_ge(bias_l1_ready, 1)
                    if part == L1:
                        bias = bias_l1[:, s * PAIR + b:s * PAIR + b + 1]
                        act.activation(probs[n % 3][:, :, :], src, ACT.Exp, bias=bias).then_inc(exp_done, 1)
                    elif part == L3C:
                        act.activation(probs[n % 3][:, :, :], src, ACT.Exp, bias=pad_bias[:, 0:1])\
                            .then_inc(exp_done, 1)
                    else:
                        act.activation(probs[n % 3][:, :, :], src, ACT.Exp).then_inc(exp_done, 1)
                if kind == "o_evac":
                    n = ub(step)
                    cols_used = HEADS[part] // 4 * P
                    last_pv = the("pv", u, b, HEADS[part] // 4 - 1)
                    act.wait_ge(pv_done, NUM[last_pv] + 1)
                    if n >= 2:
                        evacuated(act, the("o_tr", (n - 2) // PAIR, n % PAIR))
                    act.activation(o_sb[n % 2][:, 0:cols_used], o_ps[:, 0:cols_used], ACT.Copy)\
                        .then_inc(o_saved, 1)

        @block.vector
        def _(dve):
            for r in range(RING):
                dve.memset(v8[r][:, :], 1.0)
                dve.memset(v16[r][:, :], 1.0)
            for r in range(2):
                dve.memset(max_terms[r][:, :], 0.0)
            dve.wait_ge(first_landed, 48)
            for part in (L0, L1, L2):
                at = C_AT[f"bq{part}"]
                last = dve.tensor_scalar(bq_scaled[:, part:part + 1], col[:, at:at + 1],
                                         float(D // HEADS[part]) ** -0.5, None, ALU.mult)
            last.then_inc(dve_const, 1)
            for step in STEPS:
                kind, u, b, g = step
                part, s = divmod(u, SETS)
                heads = HEADS[part]
                d = D // heads
                if MISC.get(kind) == "dve":
                    dve.wait_ge(misc_ready, ORDER[step] + 1)
                    bank = misc_ps[ORDER[step] % MISC_BANKS]
                if step in LN_STEPS:
                    n = LN_STEPS.index(step)
                    if kind == "ln_in":
                        dve.wait_ge(tokens_landed[s], 32)
                        srcs = [t[s][:, k, :] for t in (x_tok, c_tok) for k in range(PAIR)]
                    else:
                        evacuated(dve, the("x_tr", u, b))
                        rows_of = x_rows[NORM_STEPS.index(the("x_norm", u, b)) % 2]
                        srcs = [rows_of[:, k * D:(k + 1) * D] for k in range(PAIR)]
                    for k, src in enumerate(srcs):
                        last = dve.bn_stats(stats[:, k, :], src)
                    last.then_inc(stats_done, 1)
                    dve.wait_ge(stats_done, n + 1)
                    for k in range(len(srcs)):
                        last = dve.bn_aggr(mean_var_ring[n % LN_RING][:, k, :], stats[:, k, :])
                    last.then_inc(var_ready, 1)
                if kind == "ln_norm":
                    n = LN_STEPS.index(the("ln_in", u))
                    dve.wait_ge(rstd_ready, n + 1)
                    if u >= 2:
                        evacuated(dve, the("ln_tr", u - 2))
                    srcs = [t[s][:, k, :] for t in (x_tok, c_tok) for k in range(PAIR)]
                    for k, src in enumerate(srcs):
                        last = dve.tensor_scalar(normed_in_ring[u % 2][:, k, :], src,
                                                 mean_var_ring[n % LN_RING][:, k, 0:1],
                                                 rstd_ring[n % LN_RING][:, k:k + 1], ALU.subtract, ALU.mult)
                    last.then_inc(input_normed, 1)
                if kind == "x_norm":
                    n = LN_STEPS.index(the("x_stats", u, b))
                    dve.wait_ge(rstd_ready, n + 1)
                    m = NORM_STEPS.index(step)
                    if m >= 2:
                        user = NORM_STEPS[m - 2]
                        if user.b == 1:
                            dve.wait_ge(y_ready, user.u % SETS + 1)
                        else:
                            evacuated(dve, the("x_back", user.u))
                    for k in range(PAIR):
                        last = dve.tensor_scalar(normed_ring[m % 2][:, k, :],
                                                 x_rows[m % 2][:, k * D:(k + 1) * D],
                                                 mean_var_ring[n % LN_RING][:, k, 0:1],
                                                 rstd_ring[n % LN_RING][:, k:k + 1], ALU.subtract, ALU.mult)
                    last.then_inc(x_normed, 1)
                if kind == "split":
                    if u >= 2:
                        stacked(dve, u - 2)
                    evacuated(dve, the("qk", u))
                    terms = terms_ring[u % 2]
                    dve.tensor_copy(terms[:, :, 0, :], qk_f32[:, :, :]).then_inc(split1_done, 1)
                if kind == "v":
                    width = PAIR * heads * (d + 1)
                    dst = v_of(u)[:, 0:width].rearrange("p (n e) -> p n e", e=d + 1)[:, :, 0:d]
                    src = bank[:, 0:TOK].rearrange("p (n e) -> p n e", e=d)
                    if part <= L2:
                        for k in range(PAIR):
                            bias = row[:, R_AT[f"bv{part}"], :].rearrange("p (n e) -> p n e", e=d)
                            last = dve.tensor_tensor(dst[:, k * heads:(k + 1) * heads, :],
                                                     src[:, k * heads:(k + 1) * heads, :], bias, ALU.add)
                    else:
                        last = dve.tensor_copy(dst, src)
                    last.then_inc(evac["dve"], 1)
                if kind == "score":
                    n = NUM[step]
                    dve.wait_ge(score_ready, n + 1)
                    dve.tensor_reduce(negmax[ub(step) % 2][:, 4 * g:4 * g + 4],
                                      score_ps[n % 2][:, :].rearrange("p (h k) -> p h k", h=4),
                                      AX_X, ALU.max, negate=True).then_inc(score_reduced, 1)
                if kind == "nmax":
                    n = ub(step)
                    nm, rm = negmax[n % 2][:, 0:heads], negmax_rest[n % 2][:, 0:heads]
                    mt = max_terms[n % 2]
                    dve.wait_ge(score_reduced, NUM[the("score", u, b, heads // 4 - 1)] + 1)
                    dve.tensor_copy(mt[:, 0:heads], nm).then_inc(term1_done, 1)
                    dve.wait_ge(term1_done, n + 1)
                    dve.tensor_tensor(rm, nm, mt[:, 0:heads], ALU.subtract).then_inc(maxrest_done, 1)
                    dve.wait_ge(maxrest_done, n + 1)
                    dve.tensor_copy(mt[:, heads:2 * heads], rm).then_inc(term2_done, 1)
                    dve.wait_ge(term2_done, n + 1)
                    dve.tensor_tensor(mt[:, 2 * heads:3 * heads], rm, mt[:, heads:2 * heads], ALU.subtract)\
                        .then_inc(maxterms_ready, 1)
                if kind == "n_tr":
                    dve.tensor_copy(max_rows[ub(step) % 4][0:TERMS * heads, :],
                                    bank[0:TERMS * heads, 0:S // 2].bitcast(BF16)).then_inc(evac["dve"], 1)
                if kind == "o_tr":
                    heads_ps = bank[:, 0:32 * heads].rearrange("p (h e) -> p h e", e=32)
                    dve.reciprocal(recip[:, 0:heads], heads_ps[:, :, d]).then_inc(recip_done, 1)
                    dve.wait_ge(recip_done, ub(step) + 1)
                    dst = attn_tok[:, b, :].rearrange("p (h e) -> p h e", e=d)
                    spread = recip[:, 0:heads].unsqueeze(2).to_broadcast([P, heads, d])
                    if part == L1:
                        at = s * PAIR + b
                        dve.scalar_tensor_tensor(dst, heads_ps[:, :, 0:d], keep_l1[:, at:at + 1], spread,
                                                 ALU.mult, ALU.mult).then_inc(evac["dve"], 1)
                    else:
                        dve.tensor_tensor(dst, heads_ps[:, :, 0:d], spread, ALU.mult).then_inc(evac["dve"], 1)
                if kind == "a_tr":
                    if part <= L1:
                        dve.tensor_tensor(xT[s][:, :], bank[:, 0:TOK], xT[s][:, :], ALU.add)\
                            .then_inc(evac["dve"], 1)
                    else:
                        dve.tensor_copy(attnT[:, :], bank[:, 0:TOK]).then_inc(evac["dve"], 1)
                if kind in ("wo", "w2"):
                    at = C_AT[f"bo{part}" if kind == "wo" else f"m2_{part}"]
                    dve.scalar_tensor_tensor(xT[s][:, :], bank[:, 0:TOK], col[:, at:at + 1], xT[s][:, :],
                                             ALU.add, ALU.add).then_inc(evac["dve"], 1)
                if kind == "x_back":
                    dve.tensor_scalar(xT[s][:, :], bank[:, 0:TOK], col[:, C_AT[f"g{part}"]:C_AT[f"g{part}"] + 1],
                                      col[:, C_AT[f"b{part}"]:C_AT[f"b{part}"] + 1], ALU.mult, ALU.add)\
                        .then_inc(evac["dve"], 1)

        @block.tensor
        def _(pe):
            pe.wait_ge(pool_const, 10)

            def weight(name):
                return w[:, W_AT[name], :]

            for step in STEPS:
                kind, u, b, g = step
                part, s = divmod(u, SETS)
                heads = HEADS[part]
                d = D // heads
                pairs = stack_of(u)
                if kind in MISC:
                    if BEFORE[step] is not None:
                        evacuated(pe, BEFORE[step])
                    bank = misc_ps[ORDER[step] % MISC_BANKS]
                if kind in ("qk", "x_tr", "w1"):
                    wrote = x_written_before(step)
                    if wrote is not None:
                        evacuated(pe, wrote)
                if kind == "raw_tr":
                    pe.wait_ge(tokens_landed[s], 32)
                    for k, src in enumerate([t[s][:, j, :] for t in (x_tok, c_tok) for j in range(PAIR)]):
                        last = pe.transpose(bank[:, k * P:(k + 1) * P], src, ident[:, :])
                    last.then_inc(misc_ready, 1)
                if kind == "ln_tr":
                    pe.wait_ge(input_normed, s + 1)
                    for k in range(2 * PAIR):
                        last = pe.transpose(bank[:, k * P:(k + 1) * P], normed_in_ring[u % 2][:, k, :], ident[:, :])
                    last.then_inc(misc_ready, 1)
                if kind == "qk":
                    if u == 0:
                        pe.wait_ge(first_landed, 48)
                    if part == L0:
                        evacuated(pe, the("ln_tr", u))
                    if u == SETS:
                        pe.wait_ge(weights_landed, 16)
                    qsrc = hT[u % 2] if part == L0 else xT[s]
                    ksrc = cnT[u % 2] if part == L0 else xT[s] if part == L3S else cT[s]
                    pe.matmul(bank[:, 0:TOK], weight(f"q{part}"), qsrc[:, :], start=True, stop=True)
                    pe.matmul(bank[:, TOK:2 * TOK], weight(f"k{part}"), ksrc[:, :], start=True, stop=True)\
                        .then_inc(misc_ready, 1)
                if kind == "v":
                    vsrc = cnT[u % 2] if part == L0 else xT[s] if part == L3S else cT[s]
                    for k in range(PAIR):
                        last = pe.matmul(bank[:, k * P:(k + 1) * P], vsrc[:, k * S:(k + 1) * S],
                                         weight(f"v{part}"), start=True, stop=True)
                    last.then_inc(misc_ready, 1)
                if kind == "score":
                    n = NUM[step]
                    if u == SETS and b == 0 and g == 0:
                        pe.wait_ge(fill16_landed, 16 * 2 * RING)
                    if b == 0 and g == 0:
                        stacked(pe, u)
                    if part == L1 and b == 0 and g == 0:
                        pe.wait_ge(mask_l1_ready, s + 1)
                    if n >= 2:
                        pe.wait_ge(score_reduced, n - 1)
                    mask = {L1: mask_l1[:, s * PAIR + b, :], L3S: mask_l3[:, :], L3C: pad_neg[:, :]}.get(part)
                    if mask is not None:
                        pe.matmul(score_ps[n % 2][:, :], ident_bf[:, :],
                                  mask.unsqueeze(1).to_broadcast([P, 4, S]), start=True, stop=False,
                                  skip_group_check=True)
                    for j in range(4):
                        h = 4 * g + j
                        last = pe.matmul(score_ps[n % 2][:, j * S:(j + 1) * S],
                                         pairs[0:STACK, h, 0, b * S:(b + 1) * S],
                                         pairs[0:STACK, h, 1, b * S:(b + 1) * S],
                                         start=mask is None, stop=True, skip_group_check=True)
                    last.then_inc(score_ready, 1)
                if kind == "n_tr":
                    m = ub(step)
                    pe.wait_ge(maxterms_ready, m + 1)
                    pe.transpose(bank[:, 0:S // 2].bitcast(BF16), max_terms[m % 2][:, :], ident_bf[:, :])\
                        .then_inc(misc_ready, 1)
                if kind == "attn":
                    n, m = NUM[step], ub(step)
                    if n == 0:
                        pe.wait_ge(fill8_landed, 16 * RING)
                    if g == 0:
                        pe.wait_ge(max_landed[m % 2], (m // 2 + 1) * 16)
                    if n >= 2:
                        pe.wait_ge(exp_done, n - 1)
                    mask = {L1: causal_t, L3S: mask_l3_t}.get(part)
                    if mask is not None:
                        pe.matmul(attn_ps[n % 2][:, :], ident_bf[:, :],
                                  mask[:, :].unsqueeze(1).to_broadcast([P, 4, S]), start=True, stop=False,
                                  skip_group_check=True)
                    for j in range(4):
                        h = 4 * g + j
                        last = pe.matmul(attn_ps[n % 2][:, j * S:(j + 1) * S],
                                         pairs[0:ROWS, h, 1, b * S:(b + 1) * S],
                                         pairs[0:ROWS, h, 0, b * S:(b + 1) * S],
                                         start=mask is None, stop=True, skip_group_check=True)
                    last.then_inc(attn_ready, 1)
                if kind == "pv":
                    n, m = NUM[step], ub(step)
                    pe.wait_ge(exp_done, n + 1)
                    if g == 0:
                        if m:
                            pe.wait_ge(o_saved, m)
                        evacuated(pe, the("v", u))
                    for j in range(4):
                        at = (b * heads + 4 * g + j) * (d + 1)
                        last = pe.matmul(o_ps[32 * j:32 * j + 32, g * P:(g + 1) * P],
                                         v_of(u)[:, at:at + 32], probs[n % 3][:, j, :],
                                         start=True, stop=True, skip_group_check=True)
                    last.then_inc(pv_done, 1)
                if kind == "o_tr":
                    pe.wait_ge(o_saved, ub(step) + 1)
                    for k in range(heads // 4):
                        last = pe.transpose(bank[:, k * P:(k + 1) * P], o_sb[ub(step) % 2][:, k * P:(k + 1) * P],
                                            ident[:, :])
                    last.then_inc(misc_ready, 1)
                if kind == "a_tr":
                    evacuated(pe, the("o_tr", u, 1))
                    for k in range(PAIR):
                        last = pe.transpose(bank[:, k * P:(k + 1) * P], attn_tok[:, k, :], ident[:, :])
                    last.then_inc(misc_ready, 1)
                if kind == "wo":
                    evacuated(pe, the("a_tr", u))
                    pe.matmul(bank[:, 0:TOK], weight(f"o{part}"), attnT[:, :], start=True, stop=True)\
                        .then_inc(misc_ready, 1)
                if kind == "w1":
                    for half in range(2):
                        last = pe.matmul(bank[:, half * TOK:(half + 1) * TOK], weight(f"w1_{part}_{2 * b + half}"),
                                         xT[s][:, :], start=True, stop=True)
                    last.then_inc(misc_ready, 1)
                if kind == "w2":
                    evacuated(pe, the("w1", u, 1))
                    for c in range(4):
                        last = pe.matmul(bank[:, 0:TOK], weight(f"w2_{part}_{c}"), hidden[:, c, :],
                                         start=(c == 0), stop=(c == 3))
                    last.then_inc(misc_ready, 1)
                if kind == "x_tr":
                    for k in range(PAIR):
                        last = pe.transpose(bank[:, k * P:(k + 1) * P], xT[s][:, k * S:(k + 1) * S], ident[:, :])
                    last.then_inc(misc_ready, 1)
                if kind == "x_back":
                    pe.wait_ge(x_normed, NORM_STEPS.index(the("x_norm", u)) + 1)
                    normed = normed_ring[NORM_STEPS.index(the("x_norm", u)) % 2]
                    for k in range(PAIR):
                        last = pe.transpose(bank[:, k * P:(k + 1) * P], normed[:, k, :], ident[:, :])
                    last.then_inc(misc_ready, 1)


def kernel(**inputs):
    import numpy as np
    import concourse.bacc as bacc
    from concourse.bass_utils import run_bass_kernel_spmd

    a = {k: np.asarray(v) for k, v in inputs.items()}

    def by_channel(m, heads):
        return m.reshape(m.shape[:-1] + (heads, D // heads)).swapaxes(-1, -2).reshape(m.shape)

    qkv = np.split(a["L3_xattn_Wqkv"], 3, axis=1)
    mats = {"o2": a["L2_xattn_Wo"], "o3": a["L3_xattn_Wo1"], "o4": a["L3_xattn_Wo2"]}
    for part, (q, k, v) in enumerate((
            [a[f"L0_xattn_W{m}"].T for m in "qkv"], [a[f"L1_xattn_W{m}"].T for m in "qkv"],
            [a[f"L2_xattn_W{m}"] for m in "qkv"], qkv, [a[f"L3_xattn_W{m}"] for m in "qkv"])):
        mats |= {f"q{part}": by_channel(q, HEADS[part]), f"k{part}": by_channel(k, HEADS[part]), f"v{part}": v}
    for part, layer in ((L2, "L2"), (L3C, "L3")):
        for c in range(4):
            mats[f"w1_{part}_{c}"] = a[f"{layer}_xattn_W1"][:, c * P:(c + 1) * P]
            mats[f"w2_{part}_{c}"] = a[f"{layer}_xattn_W2"][c * P:(c + 1) * P]
    vecs = {"ln1_w": "L0_xattn_ln1_w", "ln1_b": "L0_xattn_ln1_b", "ln2_w": "L0_xattn_ln2_w", "ln2_b": "L0_xattn_ln2_b",
            "bo2": "L2_xattn_bo", "bo3": "L3_xattn_bo1", "bo4": "L3_xattn_bo2", "m2_2": "L2_xattn_b2",
            "m2_4": "L3_xattn_bf2", "g3": "L3_xattn_g1", "b3": "L3_xattn_b1", "g4": "L3_xattn_g2",
            "b4": "L3_xattn_b2"}
    vecs = {n: a[v] for n, v in vecs.items()}
    for part in (L0, L1, L2):
        for m in "qk":
            vecs[f"b{m}{part}"] = by_channel(a[f"L{part}_xattn_b{m}"], HEADS[part])
    for c in range(4):
        vecs[f"m1_{L2}_{c}"] = a["L2_xattn_b1"][c * P:(c + 1) * P]
        vecs[f"m1_{L3C}_{c}"] = a["L3_xattn_bf1"][c * P:(c + 1) * P]
    bcast = {"bv0": a["L0_xattn_bv"], "bv1": a["L1_xattn_bv"], "bv2": a["L2_xattn_bv"],
             "g5": a["L3_xattn_g3"], "b5": a["L3_xattn_b3"]}
    valid, pad = a["mask_BxS2_bk1"], a["mask_1xS2_if1"]
    arrays = {
        "x": a["x"], "ctx": a["ctx_1024"],
        "weights": np.stack([mats[n] for n in W_NAMES], axis=1),
        "cols": np.stack([vecs[n] for n in C_NAMES], axis=1),
        "rows": np.stack([bcast[n] for n in R_NAMES]),
        "valid": valid, "valid_t": valid.T, "pad": pad[0], "pad_t": pad.T,
    }
    arrays = {f"in_{n}_dram": np.ascontiguousarray(v) for n, v in arrays.items()}
    nc = bacc.Bacc("TRN2", target_bir_lowering=False, num_devices=1)
    args = [nc.dram_tensor(n, v.shape, mybir.dt.from_np(v.dtype), kind="ExternalInput").ap()
            for n, v in arrays.items()]
    args.append(nc.dram_tensor("out_dram", (BATCHES, S, D), F32, kind="ExternalOutput").ap())
    build(nc, *args)
    result = run_bass_kernel_spmd(nc, [arrays], core_ids=[0])
    return result.results[0]["out_dram"]
```

```python
from collections import namedtuple
from contextlib import ExitStack
import math

import concourse.bass as bass
from concourse import mybir

F32 = mybir.dt.float32
BF16 = mybir.dt.bfloat16
U32 = mybir.dt.uint32
I32 = mybir.dt.int32
U8 = mybir.dt.uint8
ALU = mybir.AluOpType
ACT = mybir.ActivationFunctionType
AX_X = mybir.AxisListType.X

P = 128
BATCHES, S, D, FF = 16, 128, 128, 512
PAIR = 2
SETS = BATCHES // PAIR
TOK = PAIR * S
PARTS = 5
L0, L1, L2, L3S, L3C = range(PARTS)
HEADS = (8, 16, 16, 16, 16)
UNITS = PARTS * SETS
STACK = 96
TERMS = 3
QUARTER = 32
MASK_ROWS = S // QUARTER
SCORE_ROWS = STACK + MASK_ROWS
ROWS = SCORE_ROWS + TERMS
PRODUCTS = ((0, 0), (0, 1), (1, 0), (1, 1), (0, 2), (2, 0))
BIG = float(2 ** 100)
RING = 3
PROBS_RING = 5
LN_RING = 4
MISC_BANKS = 3
SLOT = 8
EPS_LN, EPS_LAST = 1e-5, 1e-6
GELU_SCALE, GELU_CUBE = math.sqrt(2 / math.pi), 0.044715

W_NAMES = ([f"{m}{p}" for p in range(PARTS) for m in "qkv"] + ["o2", "o3", "o4"]
           + [f"w1_{l}_{c}" for l in (2, 4) for c in range(4)] + [f"w2_{l}_{c}" for l in (2, 4) for c in range(4)])
W_AT = {n: i for i, n in enumerate(W_NAMES)}
W_FIRST = 3
C_NAMES = ["ln1_w", "ln1_b", "ln2_w", "ln2_b", "bq0", "bk0", "bq1", "bk1", "bq2", "bk2", "bo2", "bo3", "bo4",
           "m2_2", "m2_4", "g3", "b3", "g4", "b4"] + [f"m1_{l}_{c}" for l in (2, 4) for c in range(4)]
C_AT = {n: i for i, n in enumerate(C_NAMES)}
R_NAMES = ["bv0", "bv1", "bv2", "g5", "b5"]
R_AT = {n: i for i, n in enumerate(R_NAMES)}

PREPARE = {
    L0: (("load", -43), ("ln_in", -32), ("raw_tr", -30), ("ln_norm", -31), ("ln_tr", -26), ("qk", -23),
         ("split", -23), ("rest", -21), ("term1", -19), ("term2", -19), ("v", -16), ("mask", -13)),
    L1: (("qk", -22), ("split", -22), ("rest", -21), ("term1", -20), ("term2", -19), ("v", -13)),
    L2: (("qk", -21), ("split", -21), ("rest", -20), ("term1", -19), ("term2", -18), ("v", -11)),
    L3S: (("qk", -21), ("split", -21), ("rest", -19), ("term1", -18), ("term2", -17), ("v", -14)),
    L3C: (("qk", -17), ("split", -17), ("rest", -16), ("term1", -15), ("term2", -14), ("v", -13)),
}
STACK_AT = {L0: -18, L1: -15, L2: -14, L3S: -15, L3C: -15}
SCORE_AT = {L0: -9, L1: -8, L2: -8, L3S: -8, L3C: -8}
N_TR_AFTER = {L0: 2, L1: 2, L2: 2, L3S: 2, L3C: 2}
PV_AFTER = {L0: 1, L1: 2, L2: 2, L3S: 2, L3C: 2}
O_TR_AFTER = {L0: 1, L1: 1, L2: 1, L3S: 1, L3C: 1}
CHAIN = {
    L0: (("a_tr", 10),),
    L1: (("a_tr", 13),),
    L2: (("a_tr", 12), ("wo", 13), ("w1", 15), ("w1", 15), ("square", 17), ("square", 18), ("cube", 18),
         ("cube", 19), ("tanh", 21), ("tanh", 21), ("gelu", 21), ("gelu", 22), ("w2_first", 25), ("w2", 26)),
    L3S: (("a_tr", 11), ("wo", 13), ("x_tr", 16), ("x_stats", 18), ("x_norm", 19), ("x_back", 22)),
    L3C: (("a_tr", 11), ("wo", 13), ("x_tr", 14), ("x_stats", 15), ("x_norm", 17), ("x_back", 19), ("w1", 21),
          ("w1", 21), ("w2_first", 23), ("w2", 24), ("x_tr", 27), ("x_stats", 28), ("x_norm", 30), ("out", 30),
          ("store", 30)),
}

RANK = {"attn": -2, "causal": 4, "w2": 17, "score": 2, "nmax": 11, "n_tr": 15, "o_tr": 16, "load": 20, "ln_in": 20,
        "raw_tr": 20, "ln_norm": 14, "ln_tr": 2, "qk": 20, "split": 20, "rest": 20, "term1": 20, "term2": 20,
        "v": 20, "mask": 20, "stack": 20, "pv": 25, "o_evac": 2, "a_tr": 30, "wo": 30, "w1": 30, "square": 14,
        "cube": 30, "tanh": 30, "gelu": 30, "w2_first": 30, "x_tr": 30, "x_stats": 30, "x_norm": 30, "x_back": 2,
        "out": 30, "store": 30}

Step = namedtuple("Step", "kind u b g")
MISC = {"raw_tr": "act", "ln_tr": "act", "qk": "act", "v": "dve", "n_tr": "dve", "o_tr": "dve", "a_tr": "dve",
        "wo": "dve", "w1": "act", "w2": "dve", "x_tr": "act", "x_back": "dve"}


def emptied_by(step):
    plain = (step.kind == "a_tr" and step.u // SETS >= L2) or (step.kind == "v" and step.u // SETS >= L3S)
    return "act" if plain else MISC.get(step.kind)


def schedule():
    at = {}

    def put(pos, step):
        at[step.u * SLOT + pos, RANK[step.kind], len(at)] = step

    for u in range(UNITS):
        part = u // SETS
        banks = HEADS[part] // 4
        every = 4 // banks
        for kind, pos in PREPARE[part]:
            put(pos, Step(kind, u, 0, 0))
        for c in range(len(PRODUCTS)):
            put(STACK_AT[part] + c // 2, Step("stack", u, c, 0))
        for b in range(PAIR):
            for g in range(banks):
                pos = 4 * b + every * g
                put(SCORE_AT[part] + pos, Step("score", u, b, g))
                put(pos, Step("attn", u, b, g))
                if part == L1:
                    put(pos + 1, Step("causal", u, b, g))
                put(pos + PV_AFTER[part], Step("pv", u, b, g))
            last = 4 * b + every * (banks - 1)
            put(SCORE_AT[part] + last, Step("nmax", u, b, 0))
            put(SCORE_AT[part] + last + N_TR_AFTER[part], Step("n_tr", u, b, 0))
            put(last + PV_AFTER[part], Step("o_evac", u, b, 0))
            put(last + PV_AFTER[part] + O_TR_AFTER[part], Step("o_tr", u, b, 0))
        seen = {}
        for kind, pos in CHAIN[part]:
            seen[kind] = seen.get(kind, -1) + 1
            put(pos, Step(kind, u, seen[kind], 0))
    return [at[k] for k in sorted(at)]


STEPS = schedule()


def numbering():
    count, num, evac, order, before = {}, {}, {}, {}, {}
    last = [None] * MISC_BANKS
    for n, s in enumerate([s for s in STEPS if s.kind in MISC]):
        e = emptied_by(s)
        evac[s] = count.get(e, 0)
        count[e] = evac[s] + 1
        order[s], before[s] = n, last[n % MISC_BANKS]
        last[n % MISC_BANKS] = s
    for s in STEPS:
        num[s] = count.get(s.kind, 0)
        count[s.kind] = num[s] + 1
    return num, evac, order, before


NUM, EVAC, ORDER, BEFORE = numbering()
X_WRITES = [s for s in STEPS if s.kind in ("wo", "w2", "x_back") or (s.kind == "a_tr" and s.u // SETS <= L1)]
LN_STEPS = [s for s in STEPS if s.kind in ("ln_in", "x_stats")]
NORM_STEPS = [s for s in STEPS if s.kind == "x_norm"]


MASKED_ANEW = [u for u in range(SETS, UNITS) if u // SETS == L1 or u % SETS < RING]


def x_written_before(step):
    found = None
    for s in STEPS[:STEPS.index(step)]:
        if s in X_WRITES and s.u % SETS == step.u % SETS:
            found = s
    return found


def build(nc, x, ctx_in, weights, cols, rows, valid, valid_t, pad, pad_t, out):
    with ExitStack() as stack:
        def sb(name, shape, dt=F32):
            return stack.enter_context(nc.sbuf_tensor(name, shape, dt))

        def sem(name):
            return stack.enter_context(nc.semaphore(name))

        w = sb("w", [P, len(W_NAMES), P])
        col = sb("col", [P, len(C_NAMES)])
        bq_scaled = sb("bq_scaled", [P, 3])
        row = sb("row", [P, len(R_NAMES), P])
        ident = sb("ident", [P, P])
        ident_bf = sb("ident_bf", [P, P], BF16)
        causal_t = sb("causal_t", [P, S], BF16)
        valid_raw = sb("valid_raw", [P, BATCHES, S], U8)
        mask_l1 = sb("mask_l1", [P, BATCHES, S], BF16)
        validt_raw = sb("validt_raw", [P, BATCHES], U8)
        keep_l1 = sb("keep_l1", [P, BATCHES])
        pad_raw = sb("pad_raw", [P, S], I32)
        padt_raw = sb("padt_raw", [P, 1], I32)
        pad_keep = sb("pad_keep", [P, 1])
        mask_l3 = sb("mask_l3", [P, S], BF16)
        mask_l3_t = sb("mask_l3_t", [P, S], BF16)
        constant_rows = sb("constant_rows", [MASK_ROWS + TERMS, 2, PAIR, S], BF16)
        mask_rows_l1 = sb("mask_rows_l1", [MASK_ROWS, BATCHES, S], BF16)
        mask_rows_l3s = sb("mask_rows_l3s", [MASK_ROWS, PAIR, S], BF16)
        mask_rows_l3c = sb("mask_rows_l3c", [MASK_ROWS, PAIR, S], BF16)
        zero_rows = sb("zero_rows", [STACK // 2, 2 * TOK], BF16)
        minus_half = sb("minus_half", [P, 4])

        x_tok = [sb(f"x_tok{s}", [P, PAIR, D]) for s in range(SETS)]
        c_tok = [sb(f"c_tok{s}", [P, PAIR, D]) for s in range(SETS)]
        xT = [sb(f"xT{s}", [P, TOK]) for s in range(SETS)]
        cT = [sb(f"cT{s}", [P, TOK]) for s in range(SETS)]
        y = x_tok
        hT = [sb(f"hT{r}", [P, TOK]) for r in range(2)]
        cnT = [sb(f"cnT{r}", [P, TOK]) for r in range(2)]
        stats = sb("stats", [P, 2 * PAIR, 6])
        mean_var_ring = [sb(f"mean_var{r}", [P, 2 * PAIR, 2]) for r in range(LN_RING)]
        var_eps = sb("var_eps", [P, 2 * PAIR])
        rstd_ring = [sb(f"rstd{r}", [P, 2 * PAIR]) for r in range(LN_RING)]
        normed_in_ring = [sb(f"normed_in{r}", [P, 2 * PAIR, D]) for r in range(2)]
        x_rows = [sb(f"x_rows{r}", [P, TOK]) for r in range(2)]
        normed_ring = [sb(f"normed{r}", [P, PAIR, D]) for r in range(2)]
        qk_f32 = sb("qk_f32", [P, 2, TOK])
        rest = sb("rest", [P, 2, TOK])
        terms_ring = [sb(f"terms{r}", [P, 2, TERMS, TOK], BF16) for r in range(2)]
        pairs8 = [sb(f"pairs8_{r}", [P, 8, 2, TOK], BF16) for r in range(RING)]
        pairs16 = [sb(f"pairs16_{r}", [P, 16, 2, TOK], BF16) for r in range(RING)]
        v8 = [sb(f"v8_{r}", [P, PAIR * 8 * 17 + 16]) for r in range(RING)]
        v16 = [sb(f"v16_{r}", [P, PAIR * 16 + 1, 32]) for r in range(RING)]
        negmax = [sb(f"negmax{r}", [P, 16]) for r in range(2)]
        negmax_rest = [sb(f"negmax_rest{r}", [P, 16]) for r in range(2)]
        max_terms = [sb(f"max_terms{r}", [P, P], BF16) for r in range(2)]
        max_rows = [sb(f"max_rows{r}", [TERMS * 16, S], BF16) for r in range(4)]
        probs = [sb(f"probs{r}", [P, 4, S]) for r in range(PROBS_RING)]
        o_sb = [sb(f"o_sb{r}", [P, 2 * P]) for r in range(2)]
        recip = sb("recip", [P, 16])
        attn_tok = sb("attn_tok", [P, PAIR, D])
        attnT = sb("attnT", [P, TOK])
        hidden = sb("hidden", [P, 4, TOK])
        half_h = sb("half_h", [P, 4, TOK])
        gelu_arg = sb("gelu_arg", [P, 4, TOK])
        half_m1 = sb("half_m1", [P, 4])

        score_ps = [stack.enter_context(nc.psum_tensor(f"score_ps{r}", [P, 512], F32)) for r in range(2)]
        attn_ps = [stack.enter_context(nc.psum_tensor(f"attn_ps{r}", [P, 512], F32)) for r in range(2)]
        o_ps = stack.enter_context(nc.psum_tensor("o_ps", [P, 512], F32))
        misc_ps = [stack.enter_context(nc.psum_tensor(f"misc_ps{r}", [P, 512], F32)) for r in range(MISC_BANKS)]

        first_landed = sem("first_landed")
        weights_landed = sem("weights_landed")
        masks_landed = sem("masks_landed")
        tokens_landed = [sem(f"tokens_landed{s}") for s in range(SETS)]
        stack_landed = [sem(f"stack_landed{r}") for r in range(RING)]
        max_landed = [sem(f"max_landed{r}") for r in range(2)]
        out_landed = sem("out_landed")
        pool_set = sem("pool_set")
        ident_ready = sem("ident_ready")
        rows_ready = sem("rows_ready")
        mask_l3_ready = sem("mask_l3_ready")
        dve_const = sem("dve_const")
        keep_ready = sem("keep_ready")
        negated = sem("negated")
        mask_l1_ready = sem("mask_l1_ready")
        fill8_landed = sem("fill8_landed")
        mask_landed = [sem(f"mask_landed{r}") for r in range(RING)]
        fill16_landed = sem("fill16_landed")
        misc_ready = sem("misc_ready")
        evac = {"act": sem("evac_act"), "dve": sem("evac_dve")}
        score_ready = sem("score_ready")
        score_reduced = sem("score_reduced")
        term1_done = sem("term1_done")
        term2_done = sem("term2_done")
        maxterms_ready = sem("maxterms_ready")
        attn_ready = sem("attn_ready")
        exp_done = sem("exp_done")
        v_zeroed = sem("v_zeroed")
        causal_done = sem("causal_done")
        pv_done = sem("pv_done")
        o_saved = sem("o_saved")
        recip_done = sem("recip_done")
        stats_done = sem("stats_done")
        var_ready = sem("var_ready")
        eps_added = sem("eps_added")
        rstd_ready = sem("rstd_ready")
        input_normed = sem("input_normed")
        split1_done = sem("split1_done")
        split2_done = sem("split2_done")
        split_done = sem("split_done")
        scaled_g = sem("scaled_g")
        x_normed = sem("x_normed")
        square_done = sem("square_done")
        arg_done = sem("arg_done")
        tanh_done = sem("tanh_done")
        gelu_done = sem("gelu_done")
        y_ready = sem("y_ready")

        def evacuated(eng, step):
            eng.wait_ge(evac[emptied_by(step)], EVAC[step] + 1)

        def ub(s):
            return s.u * PAIR + s.b

        def stack_of(u):
            return (pairs8 if u // SETS == L0 else pairs16)[u % RING]

        def head_of(part, g, j):
            return 4 * g + j if part == L0 else 8 * (g // 2) + 2 * j + g % 2

        def v_of(u):
            return (v8 if u // SETS == L0 else v16)[u % RING]

        def stacked(eng, u):
            eng.wait_ge(stack_landed[u % RING], (u // RING + 1) * 16 * len(PRODUCTS))

        def the(kind, u, b=0, g=0):
            return Step(kind, u, b, g)

        block = stack.enter_context(nc.Block())

        @block.sync
        def _(sp):
            for step in STEPS:
                u = step.u
                part = u // SETS
                heads = HEADS[part]
                if step.kind == "load":
                    first = u * PAIR
                    sp.dma_start(x_tok[u][:, :, :], x[first:first + PAIR].rearrange("b t d -> t b d"))\
                        .then_inc(tokens_landed[u], 16)
                    sp.dma_start(c_tok[u][:, :, :], ctx_in[first:first + PAIR].rearrange("b t d -> t b d"))\
                        .then_inc(tokens_landed[u], 16)
                    if u == 0:
                        sp.dma_start(w[:, 0:W_FIRST, :], weights[:, 0:W_FIRST, :]).then_inc(first_landed, 16)
                        sp.dma_start(col[:, :], cols).then_inc(first_landed, 16)
                        sp.dma_start(row[:, :, :], rows.partition_broadcast(P)).then_inc(first_landed, 16)
                if step.kind == "load" and u == 2:
                    sp.wait_ge(rows_ready, 4)
                    for buffers, heads, landed in ((pairs8, 8, fill8_landed), (pairs16, 16, fill16_landed)):
                        for pairs in buffers:
                            sp.dma_start(pairs[STACK:ROWS, :, :, :].rearrange("p h a n -> p h (a n)"),
                                         constant_rows[:, :, :, :].rearrange("p a b n -> p (a b n)").unsqueeze(1)
                                         .to_broadcast([MASK_ROWS + TERMS, heads, 2 * TOK])).then_inc(landed, 16)
                    sp.dma_start(validt_raw[:, :], valid_t).then_inc(masks_landed, 16)
                    sp.dma_start(valid_raw[:, :, :], valid.partition_broadcast(P)).then_inc(masks_landed, 16)
                    sp.dma_start(padt_raw[:, :], pad_t).then_inc(masks_landed, 16)
                    sp.dma_start(pad_raw[:, :], pad.partition_broadcast(P)).then_inc(masks_landed, 16)
                if step.kind == "load" and u == 4:
                    sp.dma_start(w[:, W_FIRST:, :], weights[:, W_FIRST:, :]).then_inc(weights_landed, 16)
                if step.kind == "load" and u >= SETS - RING:
                    sp.dma_start(pairs16[u % RING][STACK // 2:STACK, :, :, :].rearrange("p h a n -> p h (a n)"),
                                 zero_rows[:, :].unsqueeze(1).to_broadcast([STACK // 2, 16, 2 * TOK]))\
                        .then_inc(fill16_landed, 16)
                if step.kind == "stack":
                    c = step.b
                    if c == 0:
                        sp.wait_ge(split1_done, u + 1)
                    if c == 1:
                        sp.wait_ge(split2_done, u + 1)
                    if c == 4:
                        sp.wait_ge(split_done, u + 1)
                    if c == 0:
                        if u >= RING:
                            sp.wait_ge(o_saved, (u - RING + 1) * PAIR)
                        if u == SETS:
                            sp.wait_ge(fill16_landed, 16 * 2 * RING)
                        if u in MASKED_ANEW:
                            if part == L1:
                                sp.wait_ge(mask_l1_ready, 2 * (u % SETS) + 1)
                            if u == L3S * SETS:
                                sp.wait_ge(mask_l3_ready, 1)
                            source = {L1: mask_rows_l1[:, PAIR * (u % SETS):PAIR * (u % SETS + 1), :],
                                      L2: zero_rows[0:MASK_ROWS, 0:TOK].rearrange("p (b n) -> p b n", b=PAIR),
                                      L3S: mask_rows_l3s[:, :, :], L3C: mask_rows_l3c[:, :, :]}[part]
                            sp.dma_start(stack_of(u)[STACK:SCORE_ROWS, :, 1, :],
                                         source.rearrange("p b n -> p (b n)").unsqueeze(1)
                                         .to_broadcast([MASK_ROWS, heads, TOK])).then_inc(mask_landed[u % RING], 16)
                    d = D // heads
                    tq, tk = PRODUCTS[c]
                    terms = terms_ring[u % 2]
                    gap = TERMS + tk - tq
                    sp.dma_start(stack_of(u)[c * d:(c + 1) * d, :, :, :],
                                 terms[:, :, :, :].rearrange("p a t n -> p (a t) n")[:, tq:tq + gap + 1:gap, :])\
                        .then_inc(stack_landed[u % RING], 16)
                if step.kind == "store":
                    s = u % SETS
                    sp.wait_ge(y_ready, s + 1)
                    sp.dma_start(out[s * PAIR:(s + 1) * PAIR].rearrange("b t d -> t b d"), y[s][:, :, :])\
                        .then_inc(out_landed, 16)
                if step.kind == "n_tr":
                    evacuated(sp, step)
                    n = ub(step)
                    if n == 0:
                        sp.wait_ge(fill8_landed, 16 * RING)
                    sp.dma_start(stack_of(u)[SCORE_ROWS:ROWS, :, 0, step.b * S:(step.b + 1) * S],
                                 max_rows[n % 4][0:TERMS * heads, :]).then_inc(max_landed[n % 2], 16)
            sp.wait_ge(out_landed, 16 * SETS)

        @block.gpsimd
        def _(pool):
            pool.memset(ident[:, :], 0.0).then_inc(pool_set, 1)
            pool.memset(minus_half[:, :], -0.5).then_inc(pool_set, 1)
            pool.memset(constant_rows[:, :, :, :], 1.0).then_inc(pool_set, 1)
            pool.wait_ge(pool_set, 3)
            pool.affine_select(out=ident[:, :], in_=ident[:, :], compare_op=ALU.not_equal, fill=1.0, base=0,
                               pattern=[[-1, P]], channel_multiplier=1).then_inc(ident_ready, 1)
            pool.memset(zero_rows[:, :], 0.0).then_inc(rows_ready, 1)
            pool.memset(constant_rows[0:MASK_ROWS, 1, :, :], 0.0).then_inc(rows_ready, 1)
            queries = constant_rows[0:MASK_ROWS, 0, :, :]
            pool.affine_select(out=queries, in_=queries, compare_op=ALU.is_ge, fill=0.0, base=0,
                               pattern=[[0, PAIR], [1, S]], channel_multiplier=-QUARTER).then_inc(rows_ready, 1)
            pool.wait_ge(rows_ready, 3)
            pool.affine_select(out=queries, in_=queries, compare_op=ALU.is_ge, fill=0.0, base=QUARTER - 1,
                               pattern=[[0, PAIR], [-1, S]], channel_multiplier=QUARTER).then_inc(rows_ready, 1)
            pool.wait_ge(ident_ready, 1)
            pool.tensor_copy(ident_bf[:, :], ident[:, :]).then_inc(ident_ready, 1)
            for step in STEPS:
                u = step.u
                if step.kind == "mask":
                    two = slice(PAIR * u, PAIR * (u + 1))
                    if u == 0:
                        pool.wait_ge(masks_landed, 64)
                    pool.tensor_scalar(mask_rows_l1[:, two, :], valid_raw[0:MASK_ROWS, two, :], 1.0,
                                       BIG, ALU.subtract, ALU.mult).then_inc(negated, 1)
                    pool.tensor_scalar(mask_l1[:, two, :], valid_raw[:, two, :], -BIG, None, ALU.mult)\
                        .then_inc(negated, 1)
                    pool.wait_ge(negated, 2 * (u + 1))
                    pool.affine_select(out=mask_rows_l1[:, two, :], in_=mask_rows_l1[:, two, :],
                                       compare_op=ALU.is_ge, fill=-BIG, base=QUARTER - 1,
                                       pattern=[[0, PAIR], [-1, S]], channel_multiplier=QUARTER)\
                        .then_inc(mask_l1_ready, 1)
                    pool.affine_select(out=mask_l1[:, two, :], in_=mask_l1[:, two, :], compare_op=ALU.is_ge,
                                       fill=0.0, base=-1, pattern=[[0, PAIR], [1, S]],
                                       channel_multiplier=-1).then_inc(mask_l1_ready, 1)
                if step.kind == "mask" and u == 0:
                    pool.tensor_copy(keep_l1[:, :], validt_raw[:, :]).then_inc(keep_ready, 1)
                if step.kind == "mask" and u == SETS - 1:
                    pads = pad_raw[0:MASK_ROWS, :].unsqueeze(1).to_broadcast([MASK_ROWS, PAIR, S])
                    pool.tensor_scalar(mask_rows_l3c[:, :, :], pads, 1.0, BIG, ALU.subtract, ALU.mult)\
                        .then_inc(pool_set, 1)
                    pool.tensor_scalar(mask_l3[:, :], pad_raw[:, :], -BIG, None, ALU.mult).then_inc(pool_set, 1)
                    pool.tensor_copy(pad_keep[:, :], padt_raw[:, :]).then_inc(pool_set, 1)
                    pool.memset(causal_t[:, :], 0.0).then_inc(pool_set, 1)
                    pool.wait_ge(pool_set, 7)
                    pool.affine_select(out=causal_t[:, :], in_=causal_t[:, :], compare_op=ALU.is_ge, fill=-BIG,
                                       base=0, pattern=[[1, S]], channel_multiplier=-1).then_inc(pool_set, 1)
                    pool.affine_select(out=mask_rows_l3s[:, :, :], in_=mask_rows_l3c[:, :, :],
                                       compare_op=ALU.is_ge, fill=-BIG, base=QUARTER - 1,
                                       pattern=[[0, PAIR], [-1, S]], channel_multiplier=QUARTER)\
                        .then_inc(mask_l3_ready, 1)
                    pool.affine_select(out=mask_l3[:, :], in_=mask_l3[:, :], compare_op=ALU.is_ge, fill=0.0,
                                       base=-1, pattern=[[1, S]], channel_multiplier=-1).then_inc(mask_l3_ready, 1)
                    pool.wait_ge(pool_set, 8)
                    pool.tensor_scalar(mask_l3_t[:, :], causal_t[:, :], pad_keep[:, 0:1], None, ALU.mult)\
                        .then_inc(mask_l3_ready, 1)
                if step in LN_STEPS:
                    n = LN_STEPS.index(step)
                    k = 2 * PAIR if step.kind == "ln_in" else PAIR
                    eps = EPS_LAST if step.kind == "x_stats" and step.b == 1 else EPS_LN
                    pool.wait_ge(var_ready, n + 1)
                    pool.tensor_scalar(var_eps[:, 0:k], mean_var_ring[n % LN_RING][:, 0:k, 1], eps, None, ALU.add)\
                        .then_inc(eps_added, 1)
                    pool.wait_ge(eps_added, n + 1)
                    pool.tensor_tensor(rstd_ring[n % LN_RING][:, 0:k], var_eps[:, 0:k], minus_half[:, 0:k], ALU.pow)\
                        .then_inc(rstd_ready, 1)
                terms = terms_ring[u % 2]
                if step.kind == "rest":
                    pool.wait_ge(split1_done, u + 1)
                    pool.tensor_tensor(rest[:, :, :], qk_f32[:, :, :], terms[:, :, 0, :], ALU.subtract)
                if step.kind == "term1":
                    pool.tensor_tensor(terms[:, :, 1, :], qk_f32[:, :, :], terms[:, :, 0, :], ALU.subtract)\
                        .then_inc(split2_done, 1)
                if step.kind == "term2":
                    pool.wait_ge(split2_done, u + 1)
                    pool.tensor_tensor(terms[:, :, 2, :], rest[:, :, :], terms[:, :, 1, :], ALU.subtract)\
                        .then_inc(split_done, 1)
                if step.kind == "causal":
                    n = NUM[the("attn", *step[1:])]
                    pool.wait_ge(exp_done, n + 1)
                    pool.affine_select(out=probs[n % PROBS_RING][:, :, :], in_=probs[n % PROBS_RING][:, :, :],
                                       compare_op=ALU.is_ge, fill=0.0, base=0, pattern=[[0, 4], [1, S]],
                                       channel_multiplier=-1).then_inc(causal_done, 1)
                if step.kind == "square":
                    half = slice(2 * step.b, 2 * step.b + 2)
                    evacuated(pool, the("w1", u, step.b))
                    pool.tensor_tensor(gelu_arg[:, half, :], half_h[:, half, :], half_h[:, half, :], ALU.mult)\
                        .then_inc(square_done, 1)
                if step.kind == "out":
                    s = u % SETS
                    pool.wait_ge(x_normed, NORM_STEPS.index(the("x_norm", u, 1)) + 1)
                    normed = normed_ring[NORM_STEPS.index(the("x_norm", u, 1)) % 2]
                    pool.tensor_tensor(y[s][:, :, :], normed[:, :, :],
                                       row[:, R_AT["g5"], :].unsqueeze(1).to_broadcast([P, PAIR, D]),
                                       ALU.mult).then_inc(scaled_g, 1)
                    pool.wait_ge(scaled_g, s + 1)
                    pool.tensor_tensor(y[s][:, :, :], y[s][:, :, :],
                                       row[:, R_AT["b5"], :].unsqueeze(1).to_broadcast([P, PAIR, D]),
                                       ALU.add).then_inc(y_ready, 1)

        @block.scalar
        def _(act):
            for step in STEPS:
                kind, u, b, g = step
                part, s = divmod(u, SETS)
                if emptied_by(step) == "act":
                    act.wait_ge(misc_ready, ORDER[step] + 1)
                    bank = misc_ps[ORDER[step] % MISC_BANKS]
                if kind == "raw_tr":
                    act.activation(xT[s][:, :], bank[:, 0:TOK], ACT.Copy)
                    act.activation(cT[s][:, :], bank[:, TOK:2 * TOK], ACT.Copy).then_inc(evac["act"], 1)
                if kind == "ln_tr" and u == 0:
                    act.wait_ge(first_landed, 48)
                if kind == "qk" and u == 0:
                    act.wait_ge(dve_const, 1)
                if kind == "ln_tr":
                    if u >= 2:
                        evacuated(act, the("v", u - 2))
                    act.activation(hT[u % 2][:, :], bank[:, 0:TOK], ACT.Identity,
                                   scale=col[:, C_AT["ln1_w"]:C_AT["ln1_w"] + 1],
                                   bias=col[:, C_AT["ln1_b"]:C_AT["ln1_b"] + 1])
                    act.activation(cnT[u % 2][:, :], bank[:, TOK:2 * TOK], ACT.Identity,
                                   scale=col[:, C_AT["ln2_w"]:C_AT["ln2_w"] + 1],
                                   bias=col[:, C_AT["ln2_b"]:C_AT["ln2_b"] + 1]).then_inc(evac["act"], 1)
                if kind == "qk":
                    scale = float(D // HEADS[part]) ** -0.5
                    if u:
                        act.wait_ge(split_done, u)
                    if part <= L2:
                        bk = C_AT[f"bk{part}"]
                        act.activation(qk_f32[:, 0, :], bank[:, 0:TOK], ACT.Identity, scale=scale,
                                       bias=bq_scaled[:, part:part + 1])
                        act.activation(qk_f32[:, 1, :], bank[:, TOK:2 * TOK], ACT.Identity,
                                       bias=col[:, bk:bk + 1]).then_inc(evac["act"], 1)
                    else:
                        act.activation(qk_f32[:, 0, :], bank[:, 0:TOK], ACT.Copy, scale=scale)
                        act.activation(qk_f32[:, 1, :], bank[:, TOK:2 * TOK], ACT.Copy)\
                            .then_inc(evac["act"], 1)
                if kind == "split":
                    if u >= 2:
                        stacked(act, u - 2)
                    evacuated(act, the("qk", u))
                    act.activation(terms_ring[u % 2][:, :, 0, :], qk_f32[:, :, :], ACT.Copy)\
                        .then_inc(split1_done, 1)
                if kind == "a_tr" and part >= L2:
                    if (u - 1) // SETS >= L2:
                        evacuated(act, the("wo", u - 1))
                    act.activation(attnT[:, :], bank[:, 0:TOK], ACT.Copy).then_inc(evac["act"], 1)
                if kind == "v" and part >= L3S:
                    act.wait_ge(pv_done, NUM[the("pv", u - RING, PAIR - 1, HEADS[part] // 4 - 1)] + 1)
                    d = D // HEADS[part]
                    act.activation(v_of(u)[:, 0:PAIR * HEADS[part], 16:16 + d],
                                   bank[:, 0:TOK].rearrange("p (n e) -> p n e", e=d), ACT.Copy)\
                        .then_inc(evac["act"], 1)
                if kind == "x_tr":
                    m = NORM_STEPS.index(the("x_norm", u, b))
                    if m >= 2:
                        act.wait_ge(x_normed, m - 1)
                    act.activation(x_rows[m % 2][:, :], bank[:, 0:TOK], ACT.Copy).then_inc(evac["act"], 1)
                if kind == "w1":
                    if part == L2 and s:
                        act.wait_ge(gelu_done, 2 * s)
                    if part == L3C and u % SETS:
                        evacuated(act, the("w2", u - 1))
                    for half in range(2):
                        c = 2 * b + half
                        src = bank[:, half * TOK:(half + 1) * TOK]
                        at = C_AT[f"m1_{part}_{c}"]
                        if part == L2:
                            last = act.activation(half_h[:, c, :], src, ACT.Identity, scale=0.5,
                                                  bias=half_m1[:, c:c + 1])
                        else:
                            last = act.activation(hidden[:, c, :], src, ACT.Gelu, bias=col[:, at:at + 1])
                    last.then_inc(evac["act"], 1)
                if kind == "tanh":
                    act.wait_ge(arg_done, 2 * s + b + 1)
                    act.activation(gelu_arg[:, 2 * b:2 * b + 2, :], gelu_arg[:, 2 * b:2 * b + 2, :], ACT.Tanh,
                                   scale=2 * GELU_SCALE * 4 * GELU_CUBE).then_inc(tanh_done, 1)
                if kind == "attn":
                    n = NUM[step]
                    act.wait_ge(attn_ready, n + 1)
                    if n >= PROBS_RING:
                        act.wait_ge(pv_done, n - PROBS_RING + 1)
                    src = attn_ps[n % 2][:, :].rearrange("p (h q) -> p h q", h=4)
                    act.activation(probs[n % PROBS_RING][:, :, :], src, ACT.Exp).then_inc(exp_done, 1)
                if kind == "o_evac":
                    n = ub(step)
                    last_pv = the("pv", u, b, HEADS[part] // 4 - 1)
                    act.wait_ge(pv_done, NUM[last_pv] + 1)
                    if n >= 2:
                        evacuated(act, the("o_tr", (n - 2) // PAIR, n % PAIR))
                    act.activation(o_sb[n % 2][:, :], o_ps[:, 0:2 * P], ACT.Copy)\
                        .then_inc(o_saved, 1)

        @block.vector
        def _(dve):
            for step in STEPS:
                kind, u, b, g = step
                part, s = divmod(u, SETS)
                heads = HEADS[part]
                d = D // heads
                if emptied_by(step) == "dve":
                    dve.wait_ge(misc_ready, ORDER[step] + 1)
                    bank = misc_ps[ORDER[step] % MISC_BANKS]
                if step in LN_STEPS:
                    n = LN_STEPS.index(step)
                    if kind == "ln_in":
                        dve.wait_ge(tokens_landed[s], 32)
                        srcs = [t[s][:, k, :] for t in (x_tok, c_tok) for k in range(PAIR)]
                    else:
                        evacuated(dve, the("x_tr", u, b))
                        rows_of = x_rows[NORM_STEPS.index(the("x_norm", u, b)) % 2]
                        srcs = [rows_of[:, k * D:(k + 1) * D] for k in range(PAIR)]
                    for k, src in enumerate(srcs):
                        last = dve.bn_stats(stats[:, k, :], src)
                    last.then_inc(stats_done, 1)
                    dve.wait_ge(stats_done, n + 1)
                    for k in range(len(srcs)):
                        last = dve.bn_aggr(mean_var_ring[n % LN_RING][:, k, :], stats[:, k, :])
                    last.then_inc(var_ready, 1)
                if kind == "ln_tr" and u == 0:
                    dve.wait_ge(first_landed, 48)
                    for p in (L0, L1, L2):
                        at = C_AT[f"bq{p}"]
                        dve.tensor_scalar(bq_scaled[:, p:p + 1], col[:, at:at + 1],
                                          float(D // HEADS[p]) ** -0.5, None, ALU.mult)
                    at = C_AT[f"m1_{L2}_0"]
                    dve.tensor_scalar(half_m1[:, :], col[:, at:at + 4], 0.5, None, ALU.mult).then_inc(dve_const, 1)
                if kind == "ln_in" and u == 0:
                    for ring in range(RING):
                        dve.memset(v8[ring][:, :], 1.0)
                        dve.memset(v16[ring][:, :, :], 0.0).then_inc(v_zeroed, 1)
                    for ring in range(2):
                        dve.memset(max_terms[ring][:, :], 0.0)
                    dve.wait_ge(v_zeroed, RING)
                    for ring in range(RING):
                        dve.memset(v16[ring][:, 0:PAIR * 16, 24:25], 1.0)
                if kind == "ln_norm":
                    n = LN_STEPS.index(the("ln_in", u))
                    dve.wait_ge(rstd_ready, n + 1)
                    if u >= 2:
                        evacuated(dve, the("ln_tr", u - 2))
                    srcs = [t[s][:, k, :] for t in (x_tok, c_tok) for k in range(PAIR)]
                    for k, src in enumerate(srcs):
                        last = dve.tensor_scalar(normed_in_ring[u % 2][:, k, :], src,
                                                 mean_var_ring[n % LN_RING][:, k, 0:1],
                                                 rstd_ring[n % LN_RING][:, k:k + 1], ALU.subtract, ALU.mult)
                    last.then_inc(input_normed, 1)
                if kind == "x_norm":
                    n = LN_STEPS.index(the("x_stats", u, b))
                    dve.wait_ge(rstd_ready, n + 1)
                    m = NORM_STEPS.index(step)
                    if m >= 2:
                        user = NORM_STEPS[m - 2]
                        if user.b == 1:
                            dve.wait_ge(y_ready, user.u % SETS + 1)
                        else:
                            evacuated(dve, the("x_back", user.u))
                    for k in range(PAIR):
                        last = dve.tensor_scalar(normed_ring[m % 2][:, k, :],
                                                 x_rows[m % 2][:, k * D:(k + 1) * D],
                                                 mean_var_ring[n % LN_RING][:, k, 0:1],
                                                 rstd_ring[n % LN_RING][:, k:k + 1], ALU.subtract, ALU.mult)
                    last.then_inc(x_normed, 1)
                if kind == "v" and part <= L2:
                    if u >= RING:
                        dve.wait_ge(o_saved, (u - RING + 1) * PAIR)
                    if part == L0:
                        width = PAIR * heads * (d + 1)
                        dst = v_of(u)[:, 0:width].rearrange("p (n e) -> p n e", e=d + 1)[:, :, 0:d]
                    else:
                        dst = v_of(u)[:, 0:PAIR * heads, 16:16 + d]
                    src = bank[:, 0:TOK].rearrange("p (n e) -> p n e", e=d)
                    for k in range(PAIR):
                        bias = row[:, R_AT[f"bv{part}"], :].rearrange("p (n e) -> p n e", e=d)
                        last = dve.tensor_tensor(dst[:, k * heads:(k + 1) * heads, :],
                                                 src[:, k * heads:(k + 1) * heads, :], bias, ALU.add)
                    last.then_inc(evac["dve"], 1)
                if kind == "score":
                    n = NUM[step]
                    dve.wait_ge(score_ready, n + 1)
                    dve.tensor_reduce(negmax[ub(step) % 2][:, 4 * g:4 * g + 4],
                                      score_ps[n % 2][:, :].rearrange("p (h k) -> p h k", h=4),
                                      AX_X, ALU.max, negate=True).then_inc(score_reduced, 1)
                if kind == "nmax":
                    n = ub(step)
                    nm, rm = negmax[n % 2][:, 0:heads], negmax_rest[n % 2][:, 0:heads]
                    mt = max_terms[n % 2]
                    dve.wait_ge(score_reduced, NUM[the("score", u, b, heads // 4 - 1)] + 1)
                    dve.tensor_copy(mt[:, 0:heads], nm).then_inc(term1_done, 1)
                    dve.wait_ge(term1_done, n + 1)
                    dve.tensor_tensor(rm, nm, mt[:, 0:heads], ALU.subtract)
                    dve.tensor_tensor(mt[:, heads:2 * heads], nm, mt[:, 0:heads], ALU.subtract)\
                        .then_inc(term2_done, 1)
                    dve.wait_ge(term2_done, n + 1)
                    dve.tensor_tensor(mt[:, 2 * heads:3 * heads], rm, mt[:, heads:2 * heads], ALU.subtract)\
                        .then_inc(maxterms_ready, 1)
                if kind == "n_tr":
                    dve.tensor_copy(max_rows[ub(step) % 4][0:TERMS * heads, :],
                                    bank[0:TERMS * heads, 0:S // 2].bitcast(BF16)).then_inc(evac["dve"], 1)
                if kind == "o_tr":
                    heads_ps = bank[:, 0:2 * P].rearrange("p (h e) -> p h e", h=heads)
                    dve.reciprocal(recip[:, 0:heads], heads_ps[:, :, d]).then_inc(recip_done, 1)
                    dve.wait_ge(recip_done, ub(step) + 1)
                    dst = attn_tok[:, b, :].rearrange("p (h e) -> p h e", e=d)
                    spread = recip[:, 0:heads].unsqueeze(2).to_broadcast([P, heads, d])
                    if part == L1:
                        if u == SETS and b == 0:
                            dve.wait_ge(keep_ready, 1)
                        at = s * PAIR + b
                        dve.scalar_tensor_tensor(dst, heads_ps[:, :, 0:d], keep_l1[:, at:at + 1], spread,
                                                 ALU.mult, ALU.mult).then_inc(evac["dve"], 1)
                    else:
                        dve.tensor_tensor(dst, heads_ps[:, :, 0:d], spread, ALU.mult).then_inc(evac["dve"], 1)
                if kind == "a_tr" and part <= L1:
                    dve.tensor_tensor(xT[s][:, :], bank[:, 0:TOK], xT[s][:, :], ALU.add)\
                        .then_inc(evac["dve"], 1)
                if kind in ("wo", "w2"):
                    at = C_AT[f"bo{part}" if kind == "wo" else f"m2_{part}"]
                    dve.scalar_tensor_tensor(xT[s][:, :], bank[:, 0:TOK], col[:, at:at + 1], xT[s][:, :],
                                             ALU.add, ALU.add).then_inc(evac["dve"], 1)
                half = slice(2 * b, 2 * b + 2)
                if kind == "cube":
                    dve.wait_ge(square_done, 2 * s + b + 1)
                    dve.scalar_tensor_tensor(gelu_arg[:, half, :], gelu_arg[:, half, :], 1 / (4 * GELU_CUBE),
                                             half_h[:, half, :], ALU.add, ALU.mult).then_inc(arg_done, 1)
                if kind == "gelu":
                    dve.wait_ge(tanh_done, 2 * s + b + 1)
                    if s and b == 0:
                        evacuated(dve, the("w2", u - 1))
                    dve.scalar_tensor_tensor(hidden[:, half, :], gelu_arg[:, half, :], 1.0, half_h[:, half, :],
                                             ALU.add, ALU.mult).then_inc(gelu_done, 1)
                if kind == "x_back":
                    dve.tensor_scalar(xT[s][:, :], bank[:, 0:TOK], col[:, C_AT[f"g{part}"]:C_AT[f"g{part}"] + 1],
                                      col[:, C_AT[f"b{part}"]:C_AT[f"b{part}"] + 1], ALU.mult, ALU.add)\
                        .then_inc(evac["dve"], 1)

        @block.tensor
        def _(pe):
            pe.wait_ge(ident_ready, 2)

            def weight(name):
                return w[:, W_AT[name], :]

            def diagonal(bank, mask):
                for q in range(S // QUARTER):
                    part_ = slice(q * QUARTER, (q + 1) * QUARTER)
                    pe.matmul(bank[part_, :].rearrange("p (h n) -> p h n", h=4)[:, :, part_],
                              ident_bf[part_, part_], mask[part_, part_].unsqueeze(1).to_broadcast([QUARTER, 4, QUARTER]),
                              start=True, stop=False, skip_group_check=True, tile_position=(q * QUARTER, q * QUARTER))

            for step in STEPS:
                kind, u, b, g = step
                part, s = divmod(u, SETS)
                heads = HEADS[part]
                d = D // heads
                pairs = stack_of(u)
                if kind in MISC and kind != "w2":
                    if BEFORE[step] is not None:
                        evacuated(pe, BEFORE[step])
                    bank = misc_ps[ORDER[step] % MISC_BANKS]
                if kind in ("w2_first", "w2"):
                    w2 = the("w2", u)
                    if kind == "w2_first":
                        evacuated(pe, BEFORE[w2])
                    bank = misc_ps[ORDER[w2] % MISC_BANKS]
                if kind in ("qk", "x_tr", "w1"):
                    wrote = x_written_before(step)
                    if wrote is not None:
                        evacuated(pe, wrote)
                if kind == "raw_tr":
                    pe.wait_ge(tokens_landed[s], 32)
                    for k, src in enumerate([t[s][:, j, :] for t in (x_tok, c_tok) for j in range(PAIR)]):
                        last = pe.transpose(bank[:, k * P:(k + 1) * P], src, ident[:, :])
                    last.then_inc(misc_ready, 1)
                if kind == "ln_tr":
                    pe.wait_ge(input_normed, s + 1)
                    for k in range(2 * PAIR):
                        last = pe.transpose(bank[:, k * P:(k + 1) * P], normed_in_ring[u % 2][:, k, :], ident[:, :])
                    last.then_inc(misc_ready, 1)
                if kind == "qk":
                    if u == 0:
                        pe.wait_ge(first_landed, 48)
                    if part == L0:
                        evacuated(pe, the("ln_tr", u))
                    if u == SETS:
                        pe.wait_ge(weights_landed, 16)
                    qsrc = hT[u % 2] if part == L0 else xT[s]
                    ksrc = cnT[u % 2] if part == L0 else xT[s] if part == L3S else cT[s]
                    pe.matmul(bank[:, 0:TOK], weight(f"q{part}"), qsrc[:, :], start=True, stop=True)
                    pe.matmul(bank[:, TOK:2 * TOK], weight(f"k{part}"), ksrc[:, :], start=True, stop=True)\
                        .then_inc(misc_ready, 1)
                if kind == "v":
                    vsrc = cnT[u % 2] if part == L0 else xT[s] if part == L3S else cT[s]
                    for k in range(PAIR):
                        last = pe.matmul(bank[:, k * P:(k + 1) * P], vsrc[:, k * S:(k + 1) * S],
                                         weight(f"v{part}"), start=True, stop=True)
                    last.then_inc(misc_ready, 1)
                if kind == "score":
                    n = NUM[step]
                    if u == SETS and b == 0 and g == 0:
                        pe.wait_ge(fill16_landed, 16 * 2 * RING)
                    if u == 0 and b == 0 and g == 0:
                        pe.wait_ge(fill8_landed, 16 * RING)
                    if u in MASKED_ANEW and b == 0 and g == 0:
                        earlier = len([m for m in MASKED_ANEW if m < u and m % RING == u % RING])
                        pe.wait_ge(mask_landed[u % RING], 16 * (earlier + 1))
                    if b == 0 and g == 0:
                        stacked(pe, u)
                    if u == L3S * SETS and b == 0 and g == 0:
                        pe.wait_ge(mask_l3_ready, 3)
                    if part == L1 and b == 0 and g == 0:
                        pe.wait_ge(mask_l1_ready, 2 * (s + 1))
                    if n >= 2:
                        pe.wait_ge(score_reduced, n - 1)
                    mask = {L1: mask_l1[:, s * PAIR + b, :], L3S: mask_l3[:, :]}.get(part)
                    if mask is not None:
                        diagonal(score_ps[n % 2], mask)
                    for j in range(4):
                        h = 4 * g + j
                        last = pe.matmul(score_ps[n % 2][:, j * S:(j + 1) * S],
                                         pairs[0:SCORE_ROWS, h, 0, b * S:(b + 1) * S],
                                         pairs[0:SCORE_ROWS, h, 1, b * S:(b + 1) * S],
                                         start=mask is None, stop=True, skip_group_check=True)
                    last.then_inc(score_ready, 1)
                if kind == "n_tr":
                    m = ub(step)
                    pe.wait_ge(maxterms_ready, m + 1)
                    pe.transpose(bank[:, 0:S // 2].bitcast(BF16), max_terms[m % 2][:, :], ident_bf[:, :])\
                        .then_inc(misc_ready, 1)
                if kind == "attn":
                    n, m = NUM[step], ub(step)
                    if g == 0:
                        pe.wait_ge(max_landed[m % 2], (m // 2 + 1) * 16)
                    if n >= 2:
                        pe.wait_ge(exp_done, n - 1)
                    mask = {L3S: mask_l3_t}.get(part)
                    if mask is not None:
                        diagonal(attn_ps[n % 2], mask)
                    for j in range(4):
                        h = head_of(part, g, j)
                        last = pe.matmul(attn_ps[n % 2][:, j * S:(j + 1) * S],
                                         pairs[0:ROWS, h, 1, b * S:(b + 1) * S],
                                         pairs[0:ROWS, h, 0, b * S:(b + 1) * S],
                                         start=mask is None, stop=True, skip_group_check=True)
                    last.then_inc(attn_ready, 1)
                if kind == "pv":
                    n, m = NUM[step], ub(step)
                    if part == L1:
                        pe.wait_ge(causal_done, n - NUM[the("attn", L1 * SETS)] + 1)
                    else:
                        pe.wait_ge(exp_done, n + 1)
                    if g == 0:
                        if m:
                            pe.wait_ge(o_saved, m)
                        evacuated(pe, the("v", u))
                    for j in range(4):
                        if part == L0:
                            at = (b * heads + 4 * g + j) * (d + 1)
                            values = v_of(u)[:, at:at + 32]
                        else:
                            at = (b * heads + head_of(part, g, j)) * 32 + (0 if g % 2 else 16)
                            values = v_of(u)[:, :, :].rearrange("p h e -> p (h e)")[:, at:at + 32]
                        region = g if part == L0 else g // 2
                        last = pe.matmul(o_ps[32 * j:32 * j + 32, region * P:(region + 1) * P],
                                         values, probs[n % PROBS_RING][:, j, :],
                                         start=part == L0 or g % 2 == 0, stop=True, skip_group_check=True)
                    last.then_inc(pv_done, 1)
                if kind == "o_tr":
                    pe.wait_ge(o_saved, ub(step) + 1)
                    for k in range(2):
                        last = pe.transpose(bank[:, k * P:(k + 1) * P], o_sb[ub(step) % 2][:, k * P:(k + 1) * P],
                                            ident[:, :])
                    last.then_inc(misc_ready, 1)
                if kind == "a_tr":
                    evacuated(pe, the("o_tr", u, 1))
                    for k in range(PAIR):
                        last = pe.transpose(bank[:, k * P:(k + 1) * P], attn_tok[:, k, :], ident[:, :])
                    last.then_inc(misc_ready, 1)
                if kind == "wo":
                    evacuated(pe, the("a_tr", u))
                    pe.matmul(bank[:, 0:TOK], weight(f"o{part}"), attnT[:, :], start=True, stop=True)\
                        .then_inc(misc_ready, 1)
                if kind == "w1":
                    for half in range(2):
                        last = pe.matmul(bank[:, half * TOK:(half + 1) * TOK], weight(f"w1_{part}_{2 * b + half}"),
                                         xT[s][:, :], start=True, stop=True)
                    last.then_inc(misc_ready, 1)
                if kind in ("w2_first", "w2") and part == L2:
                    pe.wait_ge(gelu_done, 2 * s + (1 if kind == "w2_first" else 2))
                if kind == "w2_first" and part == L3C:
                    evacuated(pe, the("w1", u, 1))
                if kind in ("w2_first", "w2"):
                    for c in range(2) if kind == "w2_first" else range(2, 4):
                        last = pe.matmul(bank[:, 0:TOK], weight(f"w2_{part}_{c}"), hidden[:, c, :],
                                         start=(c == 0), stop=(c == 3))
                    if kind == "w2":
                        last.then_inc(misc_ready, 1)
                if kind == "x_tr":
                    for k in range(PAIR):
                        last = pe.transpose(bank[:, k * P:(k + 1) * P], xT[s][:, k * S:(k + 1) * S], ident[:, :])
                    last.then_inc(misc_ready, 1)
                if kind == "x_back":
                    pe.wait_ge(x_normed, NORM_STEPS.index(the("x_norm", u)) + 1)
                    normed = normed_ring[NORM_STEPS.index(the("x_norm", u)) % 2]
                    for k in range(PAIR):
                        last = pe.transpose(bank[:, k * P:(k + 1) * P], normed[:, k, :], ident[:, :])
                    last.then_inc(misc_ready, 1)


def kernel(**inputs):
    import numpy as np
    import concourse.bacc as bacc
    from concourse.bass_utils import run_bass_kernel_spmd

    a = {k: np.asarray(v) for k, v in inputs.items()}

    def by_channel(m, heads):
        return m.reshape(m.shape[:-1] + (heads, D // heads)).swapaxes(-1, -2).reshape(m.shape)

    qkv = np.split(a["L3_xattn_Wqkv"], 3, axis=1)
    mats = {"o2": a["L2_xattn_Wo"], "o3": a["L3_xattn_Wo1"], "o4": a["L3_xattn_Wo2"]}
    for part, (q, k, v) in enumerate((
            [a[f"L0_xattn_W{m}"].T for m in "qkv"], [a[f"L1_xattn_W{m}"].T for m in "qkv"],
            [a[f"L2_xattn_W{m}"] for m in "qkv"], qkv, [a[f"L3_xattn_W{m}"] for m in "qkv"])):
        mats |= {f"q{part}": by_channel(q, HEADS[part]), f"k{part}": by_channel(k, HEADS[part]), f"v{part}": v}
    for part, layer in ((L2, "L2"), (L3C, "L3")):
        for c in range(4):
            mats[f"w1_{part}_{c}"] = a[f"{layer}_xattn_W1"][:, c * P:(c + 1) * P]
            mats[f"w2_{part}_{c}"] = a[f"{layer}_xattn_W2"][c * P:(c + 1) * P]
    vecs = {"ln1_w": "L0_xattn_ln1_w", "ln1_b": "L0_xattn_ln1_b", "ln2_w": "L0_xattn_ln2_w", "ln2_b": "L0_xattn_ln2_b",
            "bo2": "L2_xattn_bo", "bo3": "L3_xattn_bo1", "bo4": "L3_xattn_bo2", "m2_2": "L2_xattn_b2",
            "m2_4": "L3_xattn_bf2", "g3": "L3_xattn_g1", "b3": "L3_xattn_b1", "g4": "L3_xattn_g2",
            "b4": "L3_xattn_b2"}
    vecs = {n: a[v] for n, v in vecs.items()}
    for part in (L0, L1, L2):
        for m in "qk":
            vecs[f"b{m}{part}"] = by_channel(a[f"L{part}_xattn_b{m}"], HEADS[part])
    for c in range(4):
        vecs[f"m1_{L2}_{c}"] = a["L2_xattn_b1"][c * P:(c + 1) * P]
        vecs[f"m1_{L3C}_{c}"] = a["L3_xattn_bf1"][c * P:(c + 1) * P]
    bcast = {"bv0": a["L0_xattn_bv"], "bv1": a["L1_xattn_bv"], "bv2": a["L2_xattn_bv"],
             "g5": a["L3_xattn_g3"], "b5": a["L3_xattn_b3"]}
    valid, pad = a["mask_BxS2_bk1"], a["mask_1xS2_if1"]
    arrays = {
        "x": a["x"], "ctx": a["ctx_1024"],
        "weights": np.stack([mats[n] for n in W_NAMES], axis=1),
        "cols": np.stack([vecs[n] for n in C_NAMES], axis=1),
        "rows": np.stack([bcast[n] for n in R_NAMES]),
        "valid": valid, "valid_t": valid.T, "pad": pad[0], "pad_t": pad.T,
    }
    arrays = {f"in_{n}_dram": np.ascontiguousarray(v) for n, v in arrays.items()}
    nc = bacc.Bacc("TRN2", target_bir_lowering=False, num_devices=1)
    args = [nc.dram_tensor(n, v.shape, mybir.dt.from_np(v.dtype), kind="ExternalInput").ap()
            for n, v in arrays.items()]
    args.append(nc.dram_tensor("out_dram", (BATCHES, S, D), F32, kind="ExternalOutput").ap())
    build(nc, *args)
    result = run_bass_kernel_spmd(nc, [arrays], core_ids=[0])
    return result.results[0]["out_dram"]
```
